# Optimizing a Trainium2 kernel written in Bass

```python
import numpy as np
import jax
import jax.numpy as jnp

def _softmax(x, axis=-1):
    return jax.nn.softmax(x, axis=axis)

def _gelu(x):
    return jax.nn.gelu(x, approximate=True)

def _silu(x):
    return jax.nn.silu(x)

def _sigmoid(x):
    return jax.nn.sigmoid(x)

def _layernorm(x, axis=-1, eps=1e-05):
    m = jnp.mean(x, axis=axis, keepdims=True)
    v = jnp.var(x, axis=axis, keepdims=True)
    return (x - m) / jnp.sqrt(v + eps)

def _scatter_add(tgt, idx, src, axis=0):
    return tgt.at[idx].add(src)

def _segment_sum(src, seg, n):
    return jax.ops.segment_sum(src, seg, n)
kernel_name = 'mk_seq_postln_d1_jaxref_r8_575f05'

def setup_inputs(seed: int=0):
    np.random.seed(seed)
    _w = jnp.asarray

    def _L0_attn_setup():
        import jax, jax.numpy as jnp
        import numpy as np
        B, S, HID = (1, 128, 256)
        H, DQK, DV = (16, 128, 128)
        K = 4
        SCALE = DQK ** (-0.5)

        def _dwconv_causal(x_btc, wk, bk, seq):
            y = jax.lax.conv_general_dilated(x_btc.transpose(0, 2, 1), wk, (1,), [(K - 1, K - 1)], dimension_numbers=('NCH', 'OIH', 'NCH'), feature_group_count=wk.shape[0])
            return (y[:, :, :seq] + bk[None, :, None]).transpose(0, 2, 1)

        def _kda_forward(x, Wq, Wk, Wv, Wa, ba, Wb, bb, Wg, Wo, qc_w, qc_b, kc_w, kc_b, vc_w, vc_b, ln_g, ln_b):
            Bb, Ss, _ = x.shape
            q = x @ Wq.T
            k = x @ Wk.T
            v = x @ Wv.T
            q = jax.nn.silu(_dwconv_causal(q, qc_w, qc_b, Ss))
            k = jax.nn.silu(_dwconv_causal(k, kc_w, kc_b, Ss))
            v = jax.nn.silu(_dwconv_causal(v, vc_w, vc_b, Ss))
            q = q.reshape(Bb, Ss, H, DQK)
            k = k.reshape(Bb, Ss, H, DQK) * SCALE
            v = v.reshape(Bb, Ss, H, DV)
            a = jax.nn.sigmoid(x @ Wa.T + ba).reshape(Bb, Ss, H, DV)
            beta = jax.nn.sigmoid(x @ Wb.T + bb)

            def step(St, inp):
                kt, qt, vt, at, bt = inp
                Sk = jnp.einsum('bhij,bhj->bhi', St, kt)
                err = Sk - vt
                Sn = at[..., None] * St - (bt[..., None] * err)[..., None] * kt[:, :, None, :]
                ot = jnp.einsum('bhij,bhj->bhi', Sn, qt)
                return (Sn, ot)
            tfirst = lambda u: u.transpose(1, 0, 2, 3)
            S0 = jnp.zeros((Bb, H, DV, DQK), x.dtype)
            _, outs = jax.lax.scan(step, S0, (tfirst(k), tfirst(q), tfirst(v), tfirst(a), beta.transpose(1, 0, 2)))
            out = outs.transpose(1, 0, 2, 3)
            mu = out.mean(-1, keepdims=True)
            var = out.var(-1, keepdims=True)
            o = (out - mu) * jax.lax.rsqrt(var + 1e-05) * ln_g + ln_b
            g = jax.nn.sigmoid(x @ Wg.T).reshape(Bb, Ss, H, DV)
            o = (o * g).reshape(Bb, Ss, H * DV)
            return o @ Wo.T
        key = jax.random.key(seed)
        ks = jax.random.split(key, 12)
        w = lambda i, shape, sc=0.02: jax.random.normal(ks[i], shape, jnp.float32) * sc
        return dict(x=jax.random.normal(ks[0], (B, S, HID), jnp.float32), Wq=w(1, (H * DQK, HID)), Wk=w(2, (H * DQK, HID)), Wv=w(3, (H * DV, HID)), Wa=w(4, (H * DV, HID)), ba=jnp.zeros((H * DV,), jnp.float32), Wb=w(5, (H, HID)), bb=jnp.zeros((H,), jnp.float32), Wg=w(6, (H * DV, HID)), Wo=w(7, (HID, H * DV)), qc_w=w(8, (H * DQK, 1, K), 0.2), qc_b=jnp.zeros((H * DQK,), jnp.float32), kc_w=w(9, (H * DQK, 1, K), 0.2), kc_b=jnp.zeros((H * DQK,), jnp.float32), vc_w=w(10, (H * DV, 1, K), 0.2), vc_b=jnp.zeros((H * DV,), jnp.float32), ln_g=jnp.ones((DV,), jnp.float32), ln_b=jnp.zeros((DV,), jnp.float32))
    _L0_attn_in = _L0_attn_setup()

    def _L0_ffn_setup():
        import jax, jax.numpy as jnp
        import numpy as np
        TARGET_SPARSITY = 0.9
        LN_EPS = 1e-05

        def ternary_quant(W):
            scale = jnp.mean(jnp.abs(W))
            q = jnp.clip(jnp.round(W / (scale + 1e-08)), -1.0, 1.0) * scale
            return W + jax.lax.stop_gradient(q - W)

        def layernorm(x, gamma, beta):
            mu = jnp.mean(x, axis=-1, keepdims=True)
            var = jnp.var(x, axis=-1, keepdims=True)
            return (x - mu) * jax.lax.rsqrt(var + LN_EPS) * gamma + beta
        key = jax.random.key(seed)
        ks = jax.random.split(key, 3)
        B, S, D, N = (4, 256, 256, 1024)
        x = jax.random.normal(ks[0], (B, S, D), dtype=jnp.float32)
        W_syn = jax.random.normal(ks[1], (N, D), dtype=jnp.float32) * (1.0 / np.sqrt(D))
        b_syn = jnp.zeros((N,), dtype=jnp.float32)
        W_out = jax.random.normal(ks[2], (D, N), dtype=jnp.float32) * (1.0 / np.sqrt(N))
        b_out = jnp.zeros((D,), dtype=jnp.float32)
        gamma = jnp.ones((D,), dtype=jnp.float32)
        beta = jnp.zeros((D,), dtype=jnp.float32)
        return {'x': x, 'W_syn': W_syn, 'b_syn': b_syn, 'W_out': W_out, 'b_out': b_out, 'gamma': gamma, 'beta': beta}
    _L0_ffn_in = _L0_ffn_setup()
    _d = {'L0_attn_x': _L0_attn_in['x'], 'L0_attn_Wq': _L0_attn_in['Wq'], 'L0_attn_Wk': _L0_attn_in['Wk'], 'L0_attn_Wv': _L0_attn_in['Wv'], 'L0_attn_Wa': _L0_attn_in['Wa'], 'L0_attn_ba': _L0_attn_in['ba'], 'L0_attn_Wb': _L0_attn_in['Wb'], 'L0_attn_bb': _L0_attn_in['bb'], 'L0_attn_Wg': _L0_attn_in['Wg'], 'L0_attn_Wo': _L0_attn_in['Wo'], 'L0_attn_qc_w': _L0_attn_in['qc_w'], 'L0_attn_qc_b': _L0_attn_in['qc_b'], 'L0_attn_kc_w': _L0_attn_in['kc_w'], 'L0_attn_kc_b': _L0_attn_in['kc_b'], 'L0_attn_vc_w': _L0_attn_in['vc_w'], 'L0_attn_vc_b': _L0_attn_in['vc_b'], 'L0_attn_ln_g': _L0_attn_in['ln_g'], 'L0_attn_ln_b': _L0_attn_in['ln_b'], 'L0_ffn_W_syn': _L0_ffn_in['W_syn'], 'L0_ffn_b_syn': _L0_ffn_in['b_syn'], 'L0_ffn_W_out': _L0_ffn_in['W_out'], 'L0_ffn_b_out': _L0_ffn_in['b_out'], 'L0_ffn_gamma': _L0_ffn_in['gamma'], 'L0_ffn_beta': _L0_ffn_in['beta']}
    _x0 = _d['L0_attn_x']
    _d['L0_attn_x'] = jax.random.normal(jax.random.fold_in(jax.random.key(seed), 1), (2, 512, 256), dtype=_x0.dtype)
    del _x0
    return _d

def reference(L0_attn_x, L0_attn_Wq, L0_attn_Wk, L0_attn_Wv, L0_attn_Wa, L0_attn_ba, L0_attn_Wb, L0_attn_bb, L0_attn_Wg, L0_attn_Wo, L0_attn_qc_w, L0_attn_qc_b, L0_attn_kc_w, L0_attn_kc_b, L0_attn_vc_w, L0_attn_vc_b, L0_attn_ln_g, L0_attn_ln_b, L0_ffn_W_syn, L0_ffn_b_syn, L0_ffn_W_out, L0_ffn_b_out, L0_ffn_gamma, L0_ffn_beta):

    def _L0_attn_ref(x, Wq, Wk, Wv, Wa, ba, Wb, bb, Wg, Wo, qc_w, qc_b, kc_w, kc_b, vc_w, vc_b, ln_g, ln_b):
        import jax, jax.numpy as jnp
        import numpy as np
        B, S, HID = (1, 128, 256)
        H, DQK, DV = (16, 128, 128)
        K = 4
        SCALE = DQK ** (-0.5)

        def _dwconv_causal(x_btc, wk, bk, seq):
            y = jax.lax.conv_general_dilated(x_btc.transpose(0, 2, 1), wk, (1,), [(K - 1, K - 1)], dimension_numbers=('NCH', 'OIH', 'NCH'), feature_group_count=wk.shape[0])
            return (y[:, :, :seq] + bk[None, :, None]).transpose(0, 2, 1)

        def _kda_forward(x, Wq, Wk, Wv, Wa, ba, Wb, bb, Wg, Wo, qc_w, qc_b, kc_w, kc_b, vc_w, vc_b, ln_g, ln_b):
            Bb, Ss, _ = x.shape
            q = x @ Wq.T
            k = x @ Wk.T
            v = x @ Wv.T
            q = jax.nn.silu(_dwconv_causal(q, qc_w, qc_b, Ss))
            k = jax.nn.silu(_dwconv_causal(k, kc_w, kc_b, Ss))
            v = jax.nn.silu(_dwconv_causal(v, vc_w, vc_b, Ss))
            q = q.reshape(Bb, Ss, H, DQK)
            k = k.reshape(Bb, Ss, H, DQK) * SCALE
            v = v.reshape(Bb, Ss, H, DV)
            a = jax.nn.sigmoid(x @ Wa.T + ba).reshape(Bb, Ss, H, DV)
            beta = jax.nn.sigmoid(x @ Wb.T + bb)

            def step(St, inp):
                kt, qt, vt, at, bt = inp
                Sk = jnp.einsum('bhij,bhj->bhi', St, kt)
                err = Sk - vt
                Sn = at[..., None] * St - (bt[..., None] * err)[..., None] * kt[:, :, None, :]
                ot = jnp.einsum('bhij,bhj->bhi', Sn, qt)
                return (Sn, ot)
            tfirst = lambda u: u.transpose(1, 0, 2, 3)
            S0 = jnp.zeros((Bb, H, DV, DQK), x.dtype)
            _, outs = jax.lax.scan(step, S0, (tfirst(k), tfirst(q), tfirst(v), tfirst(a), beta.transpose(1, 0, 2)))
            out = outs.transpose(1, 0, 2, 3)
            mu = out.mean(-1, keepdims=True)
            var = out.var(-1, keepdims=True)
            o = (out - mu) * jax.lax.rsqrt(var + 1e-05) * ln_g + ln_b
            g = jax.nn.sigmoid(x @ Wg.T).reshape(Bb, Ss, H, DV)
            o = (o * g).reshape(Bb, Ss, H * DV)
            return o @ Wo.T
        return _kda_forward(x, Wq, Wk, Wv, Wa, ba, Wb, bb, Wg, Wo, qc_w, qc_b, kc_w, kc_b, vc_w, vc_b, ln_g, ln_b)

    def _L0_ffn_ref(x, W_syn, b_syn, W_out, b_out, gamma, beta):
        import jax, jax.numpy as jnp
        import numpy as np
        TARGET_SPARSITY = 0.9
        LN_EPS = 1e-05

        def ternary_quant(W):
            scale = jnp.mean(jnp.abs(W))
            q = jnp.clip(jnp.round(W / (scale + 1e-08)), -1.0, 1.0) * scale
            return W + jax.lax.stop_gradient(q - W)

        def layernorm(x, gamma, beta):
            mu = jnp.mean(x, axis=-1, keepdims=True)
            var = jnp.var(x, axis=-1, keepdims=True)
            return (x - mu) * jax.lax.rsqrt(var + LN_EPS) * gamma + beta
        B, S, D = x.shape
        N = W_syn.shape[0]
        x_flat = x.reshape(-1, D)
        z = x_flat @ ternary_quant(W_syn).T + b_syn
        k = max(1, int(N * (1.0 - TARGET_SPARSITY)))
        topv, _ = jax.lax.top_k(z, k)
        thresh = topv[:, -1:]
        hidden = jnp.where(z >= thresh, jax.nn.relu(z), 0.0)
        out = hidden @ ternary_quant(W_out).T + b_out
        out = out.reshape(B, S, D)
        return layernorm(x + out, gamma, beta)
    x = L0_attn_x
    x = _layernorm(x + _L0_attn_ref(x, L0_attn_Wq, L0_attn_Wk, L0_attn_Wv, L0_attn_Wa, L0_attn_ba, L0_attn_Wb, L0_attn_bb, L0_attn_Wg, L0_attn_Wo, L0_attn_qc_w, L0_attn_qc_b, L0_attn_kc_w, L0_attn_kc_b, L0_attn_vc_w, L0_attn_vc_b, L0_attn_ln_g, L0_attn_ln_b), axis=-1)
    x = _layernorm(x + _L0_ffn_ref(x, L0_ffn_W_syn, L0_ffn_b_syn, L0_ffn_W_out, L0_ffn_b_out, L0_ffn_gamma, L0_ffn_beta), axis=-1)
    return x

_drawn_inputs = setup_inputs


def setup_inputs(seed=0):
    import zlib

    import numpy as np

    out = dict(_drawn_inputs(seed))
    spreads = {'L0_attn_ba': (0.0, 0.8),
     'L0_attn_bb': (0.0, 0.8),
     'L0_attn_qc_b': (0.0, 0.1),
     'L0_attn_kc_b': (0.0, 0.1),
     'L0_attn_vc_b': (0.0, 0.1),
     'L0_attn_ln_g': (1.0, 0.6),
     'L0_attn_ln_b': (0.0, 0.1),
     'L0_ffn_b_syn': (0.0, 0.1),
     'L0_ffn_b_out': (0.0, 0.1),
     'L0_ffn_gamma': (1.0, 0.2),
     'L0_ffn_beta': (0.0, 0.1)}
    factors = {'L0_attn_Wa': 6.357, 'L0_attn_Wb': 5.093, 'L0_attn_Wg': 3.688}
    for name, (base, spread) in spreads.items():
        noise = np.random.default_rng([zlib.crc32(name.encode()), seed]).standard_normal(out[name].shape)
        drawn = base * np.exp(spread * noise) if base else spread * noise
        out[name] = jnp.asarray(drawn.astype(out[name].dtype))
    for name, factor in factors.items():
        out[name] = (out[name] * factor).astype(out[name].dtype)
    return out
```

```python
from contextlib import ExitStack

import numpy as np

import concourse.bass as bass
from concourse import mybir

F32 = mybir.dt.float32
ALU = mybir.AluOpType
ACT = mybir.ActivationFunctionType
AX_X = mybir.AxisListType.X

P = 128
B, S, HID = 2, 512, 256
H = 16
PAIRS = H * B
LEAF = 4
CHUNK = 32
LEAVES = CHUNK // LEAF
CHUNKS = S // CHUNK
KT = HID // P
TAPS = 4
SCALE = float(P) ** -0.5
A_FLOOR = 1e-8
LN_EPS = 1e-5
ITEMS = LEAVES * (LEAVES + 1) // 2

GROUPS = H // 2
UNITS = ["a0", "a1", "v0", "v1", "k0", "k1", "q0", "q1"]
CONVS = UNITS[2:]
GP = 4
GCOLS = GP * S


def ge(eng, sem, value):
    if isinstance(value, int) and value <= 0:
        return
    eng.wait_ge(sem, value)


class Chain:

    def __init__(self, eng, sem, per, settle=lambda: None):
        self.eng, self.sem, self.per, self.settle = eng, sem, per, settle

    def begin(self, round_):
        self.base, self.n = round_ * self.per, 0

    def __call__(self, ins):
        ins.then_inc(self.sem, 1)
        self.n += 1
        self.eng.wait_ge(self.sem, self.base + self.n)
        self.settle()

    def end(self):
        assert self.n == self.per, (self.n, self.per)


def rounds(eng, count, body):
    body(0, True, False)
    with eng.Fori(1, count - 1) as it:
        body(it, False, False)
    body(count - 1, False, True)


def project(nc, ctx, sem, block_parts, ps, din, scratch):

    def sb(name, shape):
        return ctx.enter_context(nc.sbuf_tensor(name, shape, F32))

    xT = sb("p1_xT", [P, KT, B, S])
    w = [sb(f"p1_w{i}", [P, KT, 8, P]) for i in range(2)]
    cw = [sb(f"p1_cw{i}", [P, 32]) for i in range(2)]
    wb = sb("p1_wb", [P, KT, H])
    bb = sb("p1_bb", [H, 1])
    y = [sb(f"p1_y{i}", [P, B, S]) for i in range(3)]
    k_t = [sb(f"p1_k{i}", [P, GCOLS]) for i in range(2)]
    q_t = [sb(f"p1_q{i}", [P, GCOLS]) for i in range(2)]
    nr_t = [sb(f"p1_nr{i}", [P, GCOLS]) for i in range(2)]
    ia_t = [sb(f"p1_ia{i}", [P, GCOLS]) for i in range(2)]
    ca_t = [sb(f"p1_ca{i}", [P, GCOLS]) for i in range(2)]
    j2 = sb("p1_j2", [P, GCOLS // LEAF])
    j3 = sb("p1_j3", [P, GCOLS // LEAF])
    beta = sb("p1_beta", [H, B, S])
    scrap = sb("p1_scrap", [1, 2])
    nbeta = sb("p1_nbeta", [H, CHUNKS, B, LEAF, LEAVES])

    x_loaded = sem("p1_x_loaded")
    w_loaded = [sem(f"p1_w_loaded{i}") for i in range(2)]
    projected = sem("p1_projected")
    beta_projected = sem("p1_beta_projected")
    beta_done = sem("p1_beta_done")
    nbeta_done = sem("p1_nbeta_done")
    scrap_ready = sem("p1_scrap_ready")
    sig_done = sem("p1_sig_done")
    y_done = sem("p1_y_done")
    conv_done = sem("p1_conv_done")
    silu_done = sem("p1_silu_done")
    recip_done = sem("p1_recip_done")
    dve_step = sem("p1_dve_step")
    pool_step = sem("p1_pool_step")
    pool_done = sem("p1_pool_done")
    stored = [sem(f"p1_stored{i}") for i in range(2)]
    nbeta_stored = sem("p1_nbeta_stored")
    NCONV = len(CONVS)

    def tt(tile, k):
        return tile[:, :].rearrange("p (n t) -> p n t", t=LEAF)[:, :, k]

    def sync(sp):
        sp.dma_start(xT[:, :, :, :], din["xT"]).then_inc(x_loaded, 16)
        sp.dma_start(wb[:, :, :], din["wb"]).then_inc(x_loaded, 16)
        sp.dma_start(bb[:, :], din["bb"]).then_inc(x_loaded, 16)

        def load(g, par):
            src = din["wpack"][bass.ds(g, 1)].rearrange("g p k u c -> (g p) k u c")
            sp.dma_start(w[par][:, :, :, :], src).then_inc(w_loaded[par], 16)
            sp.dma_start(cw[par][:, :], din["cpack"][bass.ds(g, 1)].rearrange("g p n -> (g p) n")).then_inc(w_loaded[par], 16)

        load(0, 0)
        load(1, 1)

        def body(it, first, last):
            for par in range(2):
                g = 2 * it + par
                sp.wait_ge(pool_done, g + 1)
                sp.wait_ge(silu_done, NCONV * g + NCONV)
                for tile, name in ((nr_t, "nr"), (ia_t, "ia"), (ca_t, "ca"), (k_t, "k"), (q_t, "q")):
                    dst = scratch[name][:, :, bass.ds(g, 1), :].rearrange("c p g n -> p c (g n)")
                    sp.dma_start(dst, tile[par][:, :].rearrange("p (c n) -> p c n", c=CHUNKS)).then_inc(stored[par], 16)
                if not last:
                    sp.wait_ge(projected, 8 * g + 8)
                    load(g + 2, par)
            if first:
                sp.wait_ge(nbeta_done, B)
                sp.dma_start(scratch["nb"].rearrange("c h n -> h c n"),
                             nbeta[:, :, :, :, :].rearrange("h c b t l -> h c (b t l)")).then_inc(nbeta_stored, 16)

        rounds(sp, GROUPS // 2, body)

    def tensor(pe):
        pe.wait_ge(x_loaded, 48)
        for b in range(B):
            for k in range(KT):
                mm = nc.tensor.matmul(ps[0:H, 6 + b, :], wb[:, k, :], xT[:, k, b, :], start=(k == 0), stop=(k == KT - 1))
        mm.then_inc(beta_projected, 1)

        def body(it, first, last):
            for par in range(2):
                g = 2 * it + par
                pe.wait_ge(w_loaded[par], 32 * it + 32)
                for u in range(8):
                    if u in (4, 5):
                        pe.wait_ge(sig_done, 2 * g + u - 3)
                    elif u in (6, 7):
                        pe.wait_ge(conv_done, NCONV * g + u - 5)
                    elif not (first and par == 0):
                        pe.wait_ge(conv_done, NCONV * (g - 1) + u + 3)
                    elif u >= 3:
                        pe.wait_ge(beta_done, 1)
                    for b in range(B):
                        for k in range(KT):
                            mm = nc.tensor.matmul(ps[:, 2 * (u % 4) + b, :], w[par][:, k, u, :], xT[:, k, b, :],
                                                  start=(k == 0), stop=(k == KT - 1))
                    mm.then_inc(projected, 1)

        rounds(pe, GROUPS // 2, body)

    def scalar(act):
        act.wait_ge(beta_projected, 1)
        nc.scalar.activation(beta[:, :, :], ps[0:H, 6:8, :], ACT.Sigmoid, bias=bb[:, 0:1]).then_inc(beta_done, 1)

        def body(it, first, last):
            for par in range(2):
                g = 2 * it + par
                ge(act, stored[par], 80 * it)
                act.wait_ge(w_loaded[par], 32 * it + 32)
                for u in range(2):
                    act.wait_ge(projected, 8 * g + u + 1)
                    out = ca_t[par][:, :].rearrange("p (c n t) -> p n c t", c=CHUNKS, t=CHUNK)[:, B * u:B * u + B]
                    nc.scalar.activation(out, ps[:, 2 * u:2 * u + 2, :].rearrange("p b (c t) -> p b c t", t=CHUNK),
                                         ACT.Sigmoid, bias=cw[par][:, 30 + u:31 + u]).then_inc(sig_done, 1)

                def tap3(n):
                    u = n + 2
                    act.wait_ge(projected, 8 * g + u + 1)
                    if not (first and par == 0 and n < 3):
                        act.wait_ge(silu_done, NCONV * g + n - 2)
                    nc.scalar.activation(y[n % 3][:, :, :], ps[:, 2 * (u % 4):2 * (u % 4) + 2, :], ACT.Identity,
                                         bias=cw[par][:, 5 * n + 4:5 * n + 5],
                                         scale=cw[par][:, 5 * n + 3:5 * n + 4]).then_inc(y_done, 1)

                def silu(n):
                    act.wait_ge(conv_done, NCONV * g + n + 1)
                    tile = {"v": nr_t, "k": k_t, "q": q_t}[CONVS[n][0]][par]
                    h = n % 2
                    out = tile[:, :].rearrange("p (c n t) -> p n c t", c=CHUNKS, t=CHUNK)[:, B * h:B * h + B]
                    nc.scalar.activation(out, y[n % 3][:, :, :].rearrange("p b (c t) -> p b c t", t=CHUNK),
                                         ACT.Silu).then_inc(silu_done, 1)

                for n in range(NCONV):
                    tap3(n)
                    if n >= 1:
                        silu(n - 1)
                silu(NCONV - 1)

        rounds(act, GROUPS // 2, body)

    def vector(dve):
        link = Chain(dve, dve_step, 2 * (1 + 2 * NCONV))

        def body(it, first, last):
            link.begin(it)
            for par in range(2):
                g = 2 * it + par
                ge(dve, stored[par], 80 * it)
                dve.wait_ge(sig_done, 2 * g + 2)
                link(nc.vector.tensor_scalar(ca_t[par][:, :], ca_t[par][:, :], A_FLOOR, None, ALU.max))
                nc.vector.reciprocal(ia_t[par][:, :], ca_t[par][:, :]).then_inc(recip_done, 1)
                for n in range(NCONV):
                    slot = 2 * ((n + 2) % 4)
                    dve.wait_ge(y_done, NCONV * g + n + 1)
                    for k in range(TAPS - 2, -1, -1):
                        s = TAPS - 1 - k
                        ins = nc.vector.scalar_tensor_tensor(
                            out=y[n % 3][:, :, s:S], in0=ps[:, slot:slot + 2, 0:S - s],
                            scalar=cw[par][:, 5 * n + k:5 * n + k + 1], in1=y[n % 3][:, :, s:S],
                            op0=ALU.mult, op1=ALU.add)
                        if k:
                            link(ins)
                        else:
                            ins.then_inc(conv_done, 1)
            link.end()

        rounds(dve, GROUPS // 2, body)

    def gpsimd(pool):
        pool.wait_ge(beta_done, 1)
        for b in range(B):
            nc.gpsimd.tensor_scalar(nbeta[:, :, b, :, :], beta[:, b, :].rearrange("h (c l t) -> h c t l", l=LEAVES, t=LEAF),
                                    -1.0, None, ALU.mult).then_inc(nbeta_done, 1)
        nc.gpsimd.memset(scrap[:, :], 0.0).then_inc(scrap_ready, 1)
        pool.wait_ge(scrap_ready, 1)

        def settle():
            nc.gpsimd.tensor_tensor(scrap[:, 0:1], scrap[:, 1:2], scrap[:, 1:2], ALU.mult)

        link = Chain(pool, pool_step, 2 * 9)

        def body(it, first, last):
            link.begin(it)
            for par in range(2):
                g = 2 * it + par
                ia, ca, nr = ia_t[par], ca_t[par], nr_t[par]
                mul = lambda o, a, b: nc.gpsimd.tensor_tensor(o, a, b, ALU.mult)
                pool.wait_ge(recip_done, g + 1)
                link(mul(j2[:, :], tt(ia, 0), tt(ia, 1)))
                link(mul(j3[:, :], j2[:, :], tt(ia, 2)))
                for k in range(1, LEAF):
                    link(mul(tt(ca, k), tt(ca, k - 1), tt(ca, k)))
                pool.wait_ge(silu_done, NCONV * g + 2)
                settle()
                link(nc.gpsimd.tensor_scalar(nr[:, :], nr[:, :], -1.0, None, ALU.mult))
                link(mul(tt(nr, 1), tt(nr, 1), tt(ia, 0)))
                link(mul(tt(nr, 2), tt(nr, 2), j2[:, :]))
                link(mul(tt(nr, 3), tt(nr, 3), j3[:, :]))
                pool.wait_ge(silu_done, NCONV * g + 4)
                settle()
                nc.gpsimd.tensor_scalar(k_t[par][:, :], k_t[par][:, :], SCALE, None, ALU.mult).then_inc(pool_done, 1)
            link.end()

        rounds(pool, GROUPS // 2, body)

    def finished(eng):
        for par in range(2):
            eng.wait_ge(stored[par], 80 * (GROUPS // 2))
        eng.wait_ge(nbeta_stored, 16)

    for name, f in (("sync", sync), ("tensor", tensor), ("scalar", scalar), ("vector", vector), ("gpsimd", gpsimd)):
        block_parts[name].append(f)
    return finished


def item(src, leaf):
    return src * LEAVES - src * (src - 1) // 2 + leaf - src


def recur(nc, ctx, sem, block_parts, ps, din, scratch, start):

    def sb(name, shape):
        return ctx.enter_context(nc.sbuf_tensor("p2_" + name, shape, F32))

    two = range(2)
    kq_st = [sb(f"kq{i}", [P, 2, PAIRS, CHUNK]) for i in two]
    ia_st, ca_st, nr_st = (sb(n, [P, PAIRS, CHUNK]) for n in ("ia", "ca", "nr"))
    nb_st = [sb(f"nb{i}", [P, LEAVES]) for i in two]
    gc = sb("gc", [P, PAIRS // 4, 2, CHUNK])
    gx = sb("gx", [P, LEAVES, 2, CHUNK])
    lm = sb("lm", [P, LEAVES, P])
    nr_lm = [sb(f"nr_lm{i}", [P, LEAVES, P]) for i in two]
    g = [sb(f"g{i}", [P, ITEMS, 2 * P]) for i in two]
    kt = [sb(f"kt{i}", [P, LEAVES, P]) for i in two]
    u = [sb(f"u{i}", [P, LEAVES, P]) for i in two]
    state = sb("state", [P, PAIRS, P])
    xs = sb("xs", [P, 2, LEAVES, P])
    us = [xs[:, 0], xs[:, 1]]
    ut = sb("ut", [P, PAIRS, CHUNK])
    nd, at, al = ([sb(f"{n}{i}", [P, LEAVES, P]) for i in two] for n in ("nd", "at", "al"))
    o = [sb(f"o{i}", [P, LEAVES, P]) for i in two]
    oc = sb("oc", [P, PAIRS, CHUNK])
    wm = sb("wm", [P, P])
    w = [sb(f"w{i}", [P, P]) for i in two]
    ab = [sb(f"ab{i}", [P, LEAVES, PAIRS]) for i in two]
    e = [sb(f"e{i}", [P, LEAVES, PAIRS]) for i in two]
    stats = sb("stats", [P, LEAVES, 6])
    mv = sb("mv", [P, LEAVES, 2])
    std, rstd, nmr = (sb(n, [P, LEAVES]) for n in ("std", "rstd", "nmr"))
    ident = sb("ident", [P, P])
    mask = sb("mask", [P, 3, P])
    em = sb("em", [P, LEAF - 1])
    scrap = sb("scrap", [1, 1])
    lngb = sb("lngb", [P, 2])
    pm = sb("pm", [P, 4])

    PK = [ps[:, 0, 0:P], ps[:, 1, 0:P]]
    PQ = [ps[:, 2, 0:P], ps[:, 3, 0:P]]
    GB = 4
    AUX = [6, 7]
    UPB = [0, 1, 4, 5]
    SPREADS = [(s, a, min(a + 4, LEAVES), q) for s in range(LEAVES) for a in range(s + 1, LEAVES, 4) for q in two]
    NG = len(SPREADS)
    G_FROM = [NG * max(0, l - 2) // (LEAVES - 2) for l in range(LEAVES + 1)]
    PREP = [("nd", 0), ("nd", 1), ("kt", 0), ("at", 0), ("at", 1), ("kt", 1), ("al", 0), ("al", 1)]

    n_ = {}
    for name, per in dict(x_mm=4, xs_ready=8, pk=4 * LEAVES, wm_ready=3 * LEAVES, w_ready=LEAVES, u_ready=LEAVES - 1,
                          ud=LEAVES - 2, pq=LEAVES, o_done=LEAVES, bn_done=LEAVES, ag_done=LEAVES, wt_mm=LEAVES,
                          wt_ev=LEAVES, ab_mm=LEAVES, ab_ev=LEAVES, prep_mm=8, prep_ev=8, gc_mm=1, gc_ev=1, g_stored=16, g_loaded=16 * LEAF, g_ev=NG, gd_ev=LEAVES, t2_mm=2,
                          us_ev=8, up_mm=8, up_ev=8, ot_mm=4, ot_ev=4, norm=LEAVES, var_ready=1, sq_ready=1,
                          rs_ready=1, nm_ready=1, ring_ready=3, nrlm_ready=1, pool_prep=1,
                          oc_stored=16, pool_step=2 * LEAVES - 2).items():
        n_[name] = (sem("p2_" + name), per)
    ldk = [sem(f"p2_ldk{i}") for i in two]
    ldg = sem("p2_ldg")
    consts = sem("p2_consts")
    zeroed = sem("p2_zeroed")
    NCONST = 5 * 16

    def wait(eng, name, c, k):
        s, per = n_[name]
        ge(eng, s, per * c + k)

    def done(ins, name):
        ins.then_inc(n_[name][0], 1)

    def rounds2(eng, prologue, chunk, epilogue):
        prologue()

        def body(it, first, last):
            for par in two:
                chunk(2 * it + par, it, par, first and par == 0, last and par == 1, last)

        rounds(eng, CHUNKS // 2, body)
        epilogue()

    def sync(sp):
        start(sp)
        for dst, src in ((ident[:, :], din["ident"]), (mask[:, :, :], din["mask"]), (em[:, :], din["em"]), (pm[:, :], din["pm"]),
                         (lngb[:, :], din["lngb"])):
            sp.dma_start(dst, src).then_inc(consts, 16)

        def at_chunk(name, c):
            return scratch[name][bass.ds(c, 1)]

        def load_kq(c, par):
            for j, name in enumerate(("k", "q")):
                sp.dma_start(kq_st[par][:, j, :, :], at_chunk(name, c).rearrange("c p g (n t) -> (c p) (g n) t", t=CHUNK)
                             ).then_inc(ldk[par], 16)
            sp.dma_start(nb_st[par][:, :], at_chunk("nb", c).rearrange("c h (m l) -> (c h m) l", l=LEAVES)
                         ).then_inc(ldk[par], 16)

        def regroup(n):
            wait(sp, "gc_ev", n, 1)
            sp.dma_start(scratch["g"].rearrange("g r n -> r g n"), gc[:, :, :, :].rearrange("p g q t -> p g (q t)")
                         ).then_inc(n_["g_stored"][0], 16)
            wait(sp, "g_stored", n, 16)
            for t in range(LEAF):
                src = scratch["g"].rearrange("g (f l t) n -> t (g f) l n", f=4, t=LEAF)[t]
                sp.dma_start(gx[t::LEAF, :, :, :].rearrange("p l q t -> p l (q t)"), src).then_inc(n_["g_loaded"][0], 16)

        def load_gates(c):
            for tile, name in ((ia_st, "ia"), (ca_st, "ca"), (nr_st, "nr")):
                sp.dma_start(tile[:, :, :], at_chunk(name, c).rearrange("c p g (n t) -> (c p) (g n) t", t=CHUNK)
                             ).then_inc(ldg, 16)

        def store(m):
            wait(sp, "ot_ev", m, 4)
            sp.dma_start(scratch["o"][bass.ds(m, 1)].rearrange("c p n t -> (c p) n t"), oc[:, :, :]
                         ).then_inc(n_["oc_stored"][0], 16)

        def prologue():
            load_kq(0, 0)
            load_gates(0)
            load_kq(1, 1)
            regroup(0)
            wait(sp, "pool_prep", 0, 1)
            wait(sp, "ring_ready", 0, 3)
            wait(sp, "nrlm_ready", 0, 1)
            load_gates(1)

        def chunk(c, it, par, first, no_next, no_load):
            if not no_load:
                wait(sp, "x_mm", c, 4)
                load_kq(c + 2, par)
            if not no_next:
                regroup(c + 1)
            if not no_load:
                wait(sp, "pool_prep", c + 1, 1)
                wait(sp, "ring_ready", c + 1, 3)
                wait(sp, "nrlm_ready", c + 1, 1)
                load_gates(c + 2)
            if not first:
                store(c - 1)

        def epilogue():
            store(CHUNKS - 1)

        rounds2(sp, prologue, chunk, epilogue)

    def gpsimd(pool):
        start(pool)
        nc.gpsimd.memset(state[:, :, :], 0.0).then_inc(zeroed, 1)
        for i in two:
            nc.gpsimd.memset(ab[i][:, 0, :], 1.0).then_inc(zeroed, 1)
        pool.wait_ge(zeroed, 3)
        pool.wait_ge(consts, NCONST)

        def prep(n, par):
            mul = lambda o_, a, b: nc.gpsimd.tensor_tensor(o_, a, b, ALU.mult)
            ge(pool, ldg, 48 * n + 48)
            wait(pool, "wt_ev", n - 2, LEAVES)
            wait(pool, "xs_ready", n - 2, 8)
            wait(pool, "ab_mm", n - 2, LEAVES)
            a_of = lambda l: ca_st[:, :, :].rearrange("p n (l t) -> p l n t", t=LEAF)[:, l, :, LEAF - 1]
            s, per = n_["pool_step"]
            k = 0

            def link(ins):
                nonlocal k
                ins.then_inc(s, 1)
                k += 1
                pool.wait_ge(s, per * n + k)

            link(mul(e[par][:, LEAVES - 1, :], a_of(LEAVES - 1), ab[par][:, 0, :]))
            for l in range(1, LEAVES):
                link(mul(ab[par][:, l, :], ab[par][:, l - 1, :], a_of(l - 1)))
                ins = mul(e[par][:, LEAVES - 1 - l, :], e[par][:, LEAVES - l, :], a_of(LEAVES - 1 - l))
                if l < LEAVES - 1:
                    link(ins)
                else:
                    done(ins, "pool_prep")
            assert k == per, (k, per)
            wait(pool, "g_loaded", n, 16 * LEAF)
            wait(pool, "pq", n - 2, LEAVES)
            for l in range(LEAVES):
                src = gx[:, l, :, LEAF * l:LEAF * l + LEAF].unsqueeze(2).broadcast_to([P, 2, PAIRS, LEAF])
                dst = g[par][:, item(l, l), :].rearrange("p (q n t) -> p q n t", q=2, t=LEAF)
                done(mul(dst, src, mask[:, 1:3, :].rearrange("p q (n t) -> p q n t", t=LEAF)), "gd_ev")

        def chunk(c, it, par, first, no_next, no_load):
            if not no_next:
                prep(c + 1, 1 - par)

        rounds2(pool, lambda: prep(0, 0), chunk, lambda: None)

    def tensor(pe):
        start(pe)
        pe.wait_ge(consts, NCONST)
        hist = []

        def aux(name, c, k):
            if len(hist) >= 2:
                wait(pe, *hist[-2])
            bank = AUX[aux.n % 2]
            aux.n += 1
            hist.append((name, c, k))
            return bank

        aux.n = 0

        def G(par, s, l, q):
            return g[par][:, item(s, l), q * P:(q + 1) * P]

        def products(n, it2, par):
            ge(pe, ldk[par], 48 * it2 + 48)
            wait(pe, "gc_ev", n, 0)
            for p in range(PAIRS):
                mm = nc.tensor.matmul(ps[32 * (p % 4):32 * (p % 4) + 32, GB, 64 * (p // 4):64 * (p // 4) + 64],
                                      kq_st[par][:, 0, p, :], kq_st[par][:, :, p, :], start=True, stop=True)
            done(mm, "gc_mm")

        def prep_job(n, par, j):
            b = aux("prep_ev", n, j + 1)
            kind, half = PREP[j]
            if kind != "kt":
                wait(pe, "ring_ready", n, ("nd", "at", "al").index(kind) + 1)
                tiles = [lm[:, 4 * half + i, :] for i in range(4)]
            else:
                ks = kq_st[par][:, 0].rearrange("p n t -> p (n t)")
                tiles = [ks[:, P * i:P * i + P] for i in range(4 * half, 4 * half + 4)]
            for i, t in enumerate(tiles):
                mm = nc.tensor.transpose(ps[:, b, i * P:(i + 1) * P], t, ident[:, :])
            done(mm, "prep_mm")

        def acc(bank, lhsT, rhs, first=False):
            return nc.tensor.matmul(bank, lhsT, rhs, start=first, stop=True, skip_group_check=True)

        def out_job(m, k):
            b = aux("ot_ev", m, k + 1)
            wait(pe, "norm", m, 2 * k + 2)
            for i in two:
                mm = nc.tensor.transpose(ps[:, b, i * P:(i + 1) * P], o_of(m)[:, 2 * k + i, :], ident[:, :])
            done(mm, "ot_mm")

        parity = {}

        def o_of(m):
            return parity["prev_o"]

        def prologue():
            pe.wait_ge(ldk[0], 48)
            products(0, 0, 0)
            for j in range(8):
                prep_job(0, 0, j)
            pe.wait_ge(zeroed, 3)

        def chunk(c, it, par, first, no_next, no_load):
            n = c + 1
            if not first:
                hist[:] = [("us_ev", c - 1, 8), ("us_ev", c - 1, 8)]
            aux.n = 0
            parity["prev_o"] = o[1 - par]
            for j in range(4):
                b = aux("xs_ready", c, 2 * j + 2)
                wait(pe, "up_ev", c - 1, 8)
                bank = ps[:, b, :].rearrange("p (n q t) -> p q n t", n=8, q=2)
                for p in range(8):
                    n2 = min(p + 2, 8)
                    mm = nc.tensor.matmul(bank[:, :, p:n2, :], state[:, 8 * j + p, :],
                                          kq_st[par][:, :, 8 * j + p:8 * j + n2, :], start=True, stop=True)
                done(mm, "x_mm")

            def base_k(l):
                wait(pe, "w_ready", c, l - 1)
                acc(PK[l % 2], xs[:, 0, l, :], ident[:, :], first=True)
                return acc(PK[l % 2], nr_lm[par][:, l, :], ident[:, :])

            def base_q(l):
                wait(pe, "o_done", c, l - 1)
                acc(PQ[l % 2], xs[:, 1, l, :], ident[:, :], first=True)

            wait(pe, "xs_ready", c, 8)
            wait(pe, "nrlm_ready", c, 1)
            done(base_k(0), "pk")
            base_q(0)
            wait(pe, "g_ev", c, NG)
            wait(pe, "gd_ev", c, LEAVES)
            for l in range(LEAVES):
                more = l + 1 < LEAVES
                uv = u[(l + 1) % 2]
                if more:
                    base_k(l + 1)
                if l >= 1:
                    b = aux("wt_ev", c, l)
                    nc.tensor.transpose(ps[:, b, 0:P], w[(l - 1) % 2][:, :], ident[:, :]).then_inc(n_["wt_mm"][0], 1)
                wait(pe, "wm_ready", c, 3 * l + 1)
                done(acc(PK[l % 2], G(par, l, l, 0), wm[:, :]), "pk")
                if not no_next:
                    prep_job(n, 1 - par, l)
                b = aux("ab_ev", c, l + 1)
                for i in range(4):
                    mm = nc.tensor.transpose(ps[:, b, i * P:(i + 1) * P],
                                             e[par][:, 0, 4 * l + i:4 * l + i + 1].broadcast_to([P, P]), ident[:, :])
                done(mm, "ab_mm")
                wait(pe, "wm_ready", c, 3 * l + 2)
                done(acc(PK[l % 2], G(par, l, l, 0), wm[:, :]), "pk")
                if more and l >= 1:
                    wait(pe, "ud", c, l)
                    for s in range(l):
                        acc(PK[(l + 1) % 2], G(par, s, l + 1, 0), uv[:, s, :])
                if not no_next and l == 0:
                    products(n, it + par, 1 - par)
                wait(pe, "wm_ready", c, 3 * l + 3)
                done(acc(PK[l % 2], G(par, l, l, 0), wm[:, :]), "pk")
                if more:
                    base_q(l + 1)
                    for s in range(l):
                        acc(PQ[(l + 1) % 2], G(par, s, l + 1, 1), uv[:, s, :])
                if l >= 4 and not first:
                    out_job(c - 1, l - 4)
                if more:
                    wait(pe, "u_ready", c, l + 1)
                    done(acc(PK[(l + 1) % 2], G(par, l, l + 1, 0), uv[:, l, :]), "pk")
                else:
                    b = aux("wt_ev", c, LEAVES)
                    wait(pe, "w_ready", c, LEAVES)
                    nc.tensor.transpose(ps[:, b, 0:P], w[l % 2][:, :], ident[:, :]).then_inc(n_["wt_mm"][0], 1)
                wait(pe, "w_ready", c, l + 1)
                done(acc(PQ[l % 2], G(par, l, l, 1), w[l % 2][:, :]), "pq")
                if more:
                    acc(PQ[(l + 1) % 2], G(par, l, l + 1, 1), uv[:, l, :])
            uf = ut[:, :, :].rearrange("p n t -> p (n t)")
            for j in two:
                b = aux("us_ev", c, 7 + j)
                wait(pe, "wt_ev", c, LEAVES)
                for i in range(4):
                    mm = nc.tensor.transpose(ps[:, b, i * P:(i + 1) * P], uf[:, (4 * j + i) * P:(4 * j + i + 1) * P],
                                             ident[:, :])
                done(mm, "t2_mm")
            if not no_next:
                wait(pe, "gc_ev", n, 1)
            for r in range(8):
                p4, half = r // 2, r % 2
                wait(pe, "us_ev", c, r + 1)
                if r >= 4:
                    wait(pe, "up_ev", c, r - 3)
                for i in range(4):
                    mm = nc.tensor.matmul(ps[:, UPB[r % 4], i * P:(i + 1) * P], kt[par][:, 4 * half + i, :],
                                          us[p4 % 2][:, 4 * half + i, :], start=True, stop=True)
                done(mm, "up_mm")

        def epilogue():
            parity["prev_o"] = o[(CHUNKS - 1) % 2]
            aux.n = 0
            for k in range(4):
                out_job(CHUNKS - 1, k)

        rounds2(pe, prologue, chunk, epilogue)

    def vector(dve):
        start(dve)
        dve.wait_ge(consts, NCONST)
        dve.wait_ge(zeroed, 3)
        mul = lambda o_, a, b: nc.vector.tensor_tensor(o_, a, b, ALU.mult)

        def spread(n, par, lo, hi):
            for s, a, b, q in SPREADS[lo:hi]:
                if lo == 0:
                    wait(dve, "g_loaded", n, 16 * LEAF)
                src = gx[:, s, q, LEAF * a:LEAF * b].rearrange("p (l t) -> p l t", t=LEAF).unsqueeze(2)
                dst = g[par][:, item(s, a):item(s, a) + b - a, q * P:(q + 1) * P].rearrange("p l (n t) -> p l n t", t=LEAF)
                own = mask[:, 0:1, :].rearrange("p o (n t) -> p o n t", t=LEAF)
                done(mul(dst, src.broadcast_to([P, b - a, PAIRS, LEAF]), own.broadcast_to([P, b - a, PAIRS, LEAF])), "g_ev")

        def outputs(c, par, l, first):
            wait(dve, "pq", c, l + 1)
            if l == 0:
                wait(dve, "ot_mm", c - 2, 4)
            done(mul(o[par][:, l, :], PQ[l % 2], at[par][:, l, :]), "o_done")
            wait(dve, "o_done", c, l + 1)
            done(nc.vector.bn_stats(stats[:, l, :], o[par][:, l, :]), "bn_done")

        def turned(c, par, l):
            wait(dve, "wt_mm", c, l + 1)
            wt = ps[:, aux_of[("wt", l)], 0:P].rearrange("p (n t) -> p n t", t=LEAF)
            done(mul(ut[:, :, LEAF * l:LEAF * l + LEAF], wt,
                     e[par][:, l, :].unsqueeze(2).broadcast_to([P, PAIRS, LEAF])), "wt_ev")

        def norm_scalars(m):
            wait(dve, "sq_ready", m, 1)
            wait(dve, "norm", m, 0)
            done(nc.vector.reciprocal(rstd[:, :], std[:, :]), "rs_ready")
            wait(dve, "rs_ready", m, 1)
            done(nc.vector.scalar_tensor_tensor(out=nmr[:, :], in0=mv[:, :, 0], scalar=-1.0, in1=rstd[:, :],
                                                op0=ALU.mult, op1=ALU.mult), "nm_ready")

        def variance(c):
            wait(dve, "bn_done", c, LEAVES)
            nc.vector.memset(scrap[:, :], 0.0)
            for l in range(LEAVES):
                done(nc.vector.bn_aggr(mv[:, l, :], stats[:, l, :]), "ag_done")
            wait(dve, "ag_done", c, LEAVES)
            done(nc.vector.tensor_scalar(std[:, :], mv[:, :, 1], LN_EPS, None, ALU.add), "var_ready")

        aux_of = {}

        def prologue():
            spread(0, 0, 0, NG)

        def chunk(c, it, par, first, no_next, no_load):
            n = c + 1
            aux_of.clear()
            aux_of.update(aux_banks(first, no_next))
            for j in range(4):
                wait(dve, "x_mm", c, j + 1)
                if j == 0:
                    wait(dve, "pool_prep", c, 1)
                bank = ps[:, aux_of[("x", j)], :].rearrange("p (n q l t) -> p q l n t", n=8, q=2, t=LEAF)
                for q in two:
                    done(mul(xs[:, q, :, 32 * j:32 * j + 32].rearrange("p l (n t) -> p l n t", t=LEAF), bank[:, q],
                             ab[par][:, :, 8 * j:8 * j + 8].unsqueeze(3).broadcast_to([P, LEAVES, 8, LEAF])), "xs_ready")
            if first:
                wait(dve, "prep_ev", 0, 8)
            else:
                wait(dve, "prep_ev", c, 8)
            for l in range(LEAVES):
                more = l + 1 < LEAVES
                for m in range(LEAF - 1):
                    wait(dve, "pk", c, 4 * l + m + 1)
                    done(nc.vector.scalar_tensor_tensor(out=wm[:, :], in0=PK[l % 2], scalar=em[:, m:m + 1],
                                                        in1=nd[par][:, l, :], op0=ALU.mult, op1=ALU.mult), "wm_ready")
                    if m == 0 and more and l >= 1:
                        wait(dve, "u_ready", c, l)
                        wait(dve, "ud", c, l - 1)
                        wait(dve, "pq", c, l)
                        done(mul(u[(l + 1) % 2][:, 0:l, :], u[l % 2][:, 0:l, :],
                                 al[par][:, l:l + 1, :].broadcast_to([P, l, P])), "ud")
                    if m == 0 and l >= 1:
                        turned(c, par, l - 1)
                    if m == 1 and l >= 1:
                        outputs(c, par, l - 1, first)
                    if m == 1 and l == 0 and not first:
                        norm_scalars(c - 1)
                    if m == 2 and not no_next:
                        spread(n, 1 - par, G_FROM[l], (G_FROM[l] + G_FROM[l + 1]) // 2)
                wait(dve, "pk", c, 4 * l + 4)
                done(mul(w[l % 2][:, :], PK[l % 2], nd[par][:, l, :]), "w_ready")
                if more:
                    wait(dve, "w_ready", c, l + 1)
                    done(mul(u[(l + 1) % 2][:, l, :], w[l % 2][:, :], al[par][:, l, :]), "u_ready")
                if not no_next:
                    spread(n, 1 - par, (G_FROM[l] + G_FROM[l + 1]) // 2, G_FROM[l + 1])
                wait(dve, "ab_mm", c, l + 1)
                done(mul(state[:, 4 * l:4 * l + 4, :], state[:, 4 * l:4 * l + 4, :],
                         ps[:, aux_of[("ab", l)], :].rearrange("p (n i) -> p n i", n=4)), "ab_ev")
            turned(c, par, LEAVES - 1)
            outputs(c, par, LEAVES - 1, first)
            variance(c)
            wait(dve, "ab_ev", c, LEAVES)
            by4 = state[:, :, :].rearrange("p (n f) i -> p n f i", f=4)
            for r in range(8):
                wait(dve, "up_mm", c, r + 1)
                st = by4[:, 4 * (r % 2):4 * (r % 2) + 4, r // 2, :]
                done(nc.vector.tensor_tensor(st, st, ps[:, UPB[r % 4], :].rearrange("p (n i) -> p n i", n=4),
                                             ALU.add), "up_ev")

        def epilogue():
            norm_scalars(CHUNKS - 1)

        rounds2(dve, prologue, chunk, epilogue)

    def scalar(act):
        start(act)
        act.wait_ge(consts, NCONST)
        aux_of = {}

        def prep_read(n, it2, par, j, bank):
            wait(act, "prep_mm", n, j + 1)
            if j == 0:
                wait(act, "o_done", n - 2, LEAVES)
                wait(act, "up_mm", n - 2, 8)
            src = ps[:, bank, :].rearrange("p (n i) -> p n i", n=4)
            kind, half = PREP[j]
            part = slice(4 * half, 4 * half + 4)
            if kind == "nd":
                for i in range(4):
                    l = 4 * half + i
                    ins = nc.scalar.activation(nd[par][:, l, :], src[:, i, :], ACT.Copy, scale=nb_st[par][:, l:l + 1])
            else:
                tile = dict(at=at, al=al, kt=kt)[kind]
                ins = nc.scalar.activation(tile[par][:, part, :], src, ACT.Copy)
            done(ins, "prep_ev")

        def by_leaf(tile):
            return tile.rearrange("p n (l t) -> p l n t", t=LEAF)

        def to_leaves(dst, src, name):
            done(nc.scalar.activation(dst[:, :, :].rearrange("p l (n t) -> p l n t", t=LEAF), src, ACT.Copy), name)

        def prep_step(n, it2, par, j, bank):
            if j == 0:
                ge(act, ldk[par], 48 * it2 + 48)
                ge(act, ldg, 48 * n + 48)
                wait(act, "prep_mm", n - 1, 8)
                to_leaves(lm, by_leaf(ia_st[:, :, :]), "ring_ready")
            prep_read(n, it2, par, j, bank)
            if j == 0:
                wait(act, "gc_mm", n, 1)
                wait(act, "g_stored", n, 0)
                done(nc.scalar.activation(gc[:, :, :, :].rearrange("p g q t -> p (g q t)"), ps[:, GB, :], ACT.Copy), "gc_ev")
            if j == 1:
                wait(act, "prep_mm", n, 2)
                to_leaves(lm, by_leaf(ca_st[:, :, :]), "ring_ready")
            if j == 2:
                wait(act, "pk", n - 2, 4 * LEAVES)
                to_leaves(nr_lm[par], by_leaf(nr_st[:, :, :]), "nrlm_ready")
            if j == 4:
                wait(act, "prep_mm", n, 5)
                last = by_leaf(ca_st[:, :, :])[:, :, :, LEAF - 1:LEAF]
                to_leaves(lm, last.broadcast_to([P, LEAVES, PAIRS, LEAF]), "ring_ready")

        def root(m):
            wait(act, "var_ready", m, 1)
            done(nc.scalar.activation(std[:, :], std[:, :], ACT.Sqrt), "sq_ready")

        def normalise(m, tile, lo, hi):
            wait(act, "nm_ready", m, 1)
            for l in range(lo, hi):
                done(nc.scalar.activation(tile[:, l, :], tile[:, l, :], ACT.Identity, scale=rstd[:, l:l + 1],
                                          bias=nmr[:, l:l + 1]), "norm")

        def out_read(m, k, bank):
            wait(act, "ot_mm", m, k + 1)
            if k == 0:
                wait(act, "oc_stored", m, 0)
            dst = oc[:, :, :].rearrange("p n (l t) -> p l n t", t=LEAF)[:, 2 * k:2 * k + 2]
            done(nc.scalar.activation(dst, ps[:, bank, 0:2 * P].rearrange("p (l n t) -> p l n t", l=2, t=LEAF),
                                      ACT.Identity, scale=lngb[:, 0:1], bias=lngb[:, 1:2]), "ot_ev")

        def prologue():
            for j in range(8):
                prep_step(0, 0, 0, j, AUX[j % 2])

        def chunk(c, it, par, first, no_next, no_load):
            aux_of.clear()
            aux_of.update(aux_banks(first, no_next))
            for l in range(LEAVES):
                if not no_next:
                    prep_step(c + 1, it + par, 1 - par, l, aux_of[("prep", l)])
                if not first:
                    if l == 0:
                        root(c - 1)
                    if 1 <= l < 4:
                        normalise(c - 1, o[1 - par], (0, 3, 6)[l - 1], (3, 6, 8)[l - 1])
                    if l >= 4:
                        out_read(c - 1, l - 4, aux_of[("ot", l - 4)])
            for r in range(8):
                p4, half = r // 2, r % 2
                if r < 2:
                    wait(act, "t2_mm", c, r + 1)
                if r >= 4:
                    wait(act, "up_mm", c, r - 3)
                done(nc.scalar.activation(us[p4 % 2][:, 4 * half:4 * half + 4, :],
                                          ps[:, aux_of[("t2", half)], :].rearrange("p (n i) -> p n i", n=4),
                                          ACT.Copy, scale=pm[:, p4:p4 + 1]), "us_ev")

        def epilogue():
            root(CHUNKS - 1)
            normalise(CHUNKS - 1, o[(CHUNKS - 1) % 2], 0, LEAVES)
            for k in range(4):
                out_read(CHUNKS - 1, k, AUX[k % 2])

        rounds2(act, prologue, chunk, epilogue)

    def aux_jobs(first, no_next):
        jobs = [("x", j) for j in range(4)]
        for l in range(LEAVES):
            if l >= 1:
                jobs.append(("wt", l - 1))
            if not no_next:
                jobs.append(("prep", l))
            jobs.append(("ab", l))
            if l >= 4 and not first:
                jobs.append(("ot", l - 4))
        jobs += [("wt", LEAVES - 1), ("t2", 0), ("t2", 1)]
        return jobs

    assert all(len(aux_jobs(*kind)) % 2 == 0 for kind in ((True, False), (False, False), (False, True)))

    def aux_banks(first, no_next):
        return {job: AUX[i % 2] for i, job in enumerate(aux_jobs(first, no_next))}

    for name, f in (("sync", sync), ("tensor", tensor), ("scalar", scalar), ("vector", vector), ("gpsimd", gpsimd)):
        block_parts[name].append(f)

    def finished(eng):
        eng.wait_ge(n_["oc_stored"][0], 16 * CHUNKS)
    return finished


TILES = B * S // P
FF = 1024
TOPK = max(1, int(FF * (1.0 - 0.9)))
FT = FF // P
ROUNDS_MAX = (TOPK + 7) // 8


def finish(nc, ctx, sem, block_parts, ps, din, scratch, out, start):

    def sb(name, shape):
        return ctx.enter_context(nc.sbuf_tensor("p3_" + name, shape, F32))

    two = range(2)
    wg = sb("wg", [P, KT, H, P])
    wo = sb("wo", [P, H, HID])
    wt = [sb("wsyn", [P, 2048]), sb("wout", [P, 2048])]
    tmp = [sb(f"tmp{i}", [P, 2048]) for i in two]
    asum = sb("asum", [P, 2])
    thr = sb("thr", [P, 3, 2])
    xt = [sb(f"xt{i}", [P, KT, P]) for i in two]
    xr = [sb(f"xr{i}", [P, HID]) for i in two]
    ot = [sb(f"ot{i}", [P, 2, H, B * CHUNK]) for i in two]
    gt = sb("gt", [P, H, P])
    og = sb("og", [P, H, P])
    bsyn = sb("bsyn", [1, FF])
    bout = sb("bout", [1, HID])
    gam, bet = sb("gam", [P, HID]), sb("bet", [P, HID])
    ones = sb("ones", [P, P])
    ident = sb("ident", [P, P])
    r1 = sb("r1", [P, HID])
    x1 = [sb(f"x1{i}", [P, HID]) for i in two]
    x1t = sb("x1t", [P, KT, P])
    z = [sb(f"z{i}", [P, FF]) for i in two]
    zr = [sb(f"zr{i}", [P, FF]) for i in two]
    zw = sb("zw", [P, FF])
    top = sb("top", [P, ROUNDS_MAX, 8])
    scrap = sb("scrap", [1, 1])
    hid = sb("hid", [P, FF])
    ht = sb("ht", [P, FT, P])
    r2, y2 = sb("r2", [P, HID]), sb("y2", [P, HID])
    res = [sb(f"res{i}", [P, HID]) for i in two]
    stats, mv, sd, rs = (sb(n, [P, 3, k]) for n, k in (("stats", 6), ("mv", 2), ("sd", 1), ("rs", 1)))

    n_ = {}
    for name, per in dict(g_mm=4, g_ev=4, og_done=2, attn=1, r1_done=1, x1_done=1, xt_mm=1, xt_ev=1, z_mm=2, z_ev=2,
                          zr_ev=2, hid_done=1, ht_mm=2, ht_ev=2, out_mm=1, r2_done=1, var=1, root=1, bvar=2, broot=2,
                          res_done=1, fstep=3, bstep=2 * ROUNDS_MAX - 1 + 10).items():
        n_[name] = (sem("p3_" + name), per)
    wl = sem("p3_weights")
    ld = [sem(f"p3_ld{i}") for i in two]
    st = [sem(f"p3_st{i}") for i in two]
    absd, tot, ready, qstep, ternary = (sem("p3_" + n) for n in ("absd", "tot", "ready", "qstep", "ternary"))
    loads = [(wt[0][:, :], "wsynT"), (wt[1][:, :], "woutT"), (wg[:, :, :, :], "wgT"), (wo[:, :, :], "woT"),
             (bsyn[:, :], "bsyn"), (bout[:, :], "bout"), (gam[:, :], "gam"), (bet[:, :], "bet"), (ident[:, :], "ident")]
    NW = 16 * len(loads)

    def wait(eng, name, n, k):
        s, per = n_[name]
        ge(eng, s, per * n + k)

    def done(ins, name):
        ins.then_inc(n_[name][0], 1)

    def tiles(eng, prologue, tile):
        prologue()

        def body(it, first, last):
            for par in two:
                tile(2 * it + par, it, par, last and par == 1, last)

        rounds(eng, TILES // 2, body)

    def sync(sp):
        start(sp)
        for dst, name in loads:
            src = din[name]
            if name in ("gam", "bet"):
                src = src.broadcast_to([P, HID])
            sp.dma_start(dst, src).then_inc(wl, 16)

        def load(n, par):
            xsrc = din["xT"].rearrange("p k b (n c t) -> n p k c b t", c=2, t=CHUNK)
            for c in two:
                for k in range(KT):
                    sp.dma_start(xt[par][:, k, c * 64:c * 64 + 64].rearrange("p (b t) -> p b t", b=B),
                                 xsrc[bass.ds(n, 1), :, k, c].rearrange("n p b t -> (n p) b t")).then_inc(ld[par], 16)
                for b in range(B):
                    sp.dma_start(xr[par][c * 64 + b * 32:c * 64 + b * 32 + 32, :],
                                 din["x"].rearrange("b (n c t) d -> b c n t d", c=2, t=CHUNK)[b, c, bass.ds(n, 1)]
                                 .rearrange("n t d -> (n t) d")).then_inc(ld[par], 16)
                sp.dma_start(ot[par][:, c, :, :], scratch["o"].rearrange("(n c) p (h b) t -> n c p h (b t)", c=2, b=B)
                             [bass.ds(n, 1), c].rearrange("n p h t -> (n p) h t")).then_inc(ld[par], 16)

        def tile(n, it, par, no_next, no_load):
            if not no_load:
                wait(sp, "r1_done", n, 1)
                wait(sp, "og_done", n, 2)
                wait(sp, "g_mm", n, 4)
                load(n + 2, par)
            wait(sp, "res_done", n, 1)
            for c in two:
                for b in range(B):
                    sp.dma_start(out.rearrange("b (n c t) d -> b c n t d", c=2, t=CHUNK)[b, c, bass.ds(n, 1)]
                                 .rearrange("n t d -> (n t) d"),
                                 res[par][c * 64 + b * 32:c * 64 + b * 32 + 32, :]).then_inc(st[par], 16)

        def prologue():
            load(0, 0)
            load(1, 1)

        tiles(sp, prologue, tile)
        for par in two:
            sp.wait_ge(st[par], 64 * (TILES // 2))

    NLD = 16 * 10

    def tensor(pe):
        start(pe)
        pe.wait_ge(wl, NW)
        pe.wait_ge(ready, 1)
        pe.wait_ge(absd, 2)
        nc.tensor.matmul(ps[:, 7, 0:2], ones[:, :], asum[:, :], start=True, stop=True).then_inc(tot, 1)

        def attend(n, it, par):
            ge(pe, ld[par], NLD * it + NLD)
            for j in range(4):
                wait(pe, "g_ev", n, j - 1)
                for i in range(4):
                    for k in range(KT):
                        mm = nc.tensor.matmul(ps[:, j % 2, i * P:(i + 1) * P], wg[:, k, 4 * j + i, :], xt[par][:, k, :],
                                              start=(k == 0), stop=(k == KT - 1))
                done(mm, "g_mm")
            wait(pe, "og_done", n, 2)
            wait(pe, "r1_done", n, 0)
            for h in range(H):
                mm = nc.tensor.matmul(ps[:, 2, 0:HID], og[:, h, :], wo[:, h, :], start=(h == 0), stop=(h == H - 1))
            done(mm, "attn")

        def front(n, par, first):
            wait(pe, "x1_done", n, 1)
            wait(pe, "ht_ev", n - 1, 0)
            for k in range(KT):
                mm = nc.tensor.transpose(ps[:, 5, k * P:(k + 1) * P], x1[par][:, k * P:(k + 1) * P], ident[:, :])
            done(mm, "xt_mm")
            wait(pe, "xt_ev", n, 1)
            if first:
                pe.wait_ge(ternary, 1)
            for half in two:
                wait(pe, "zr_ev", n - 1, half + 1)
                cols = slice(512 * half, 512 * half + 512)
                for k in range(KT):
                    nc.tensor.matmul(ps[:, 3 + half, :], x1t[:, k, :],
                                     wt[0][:, :].rearrange("p (k n) -> p k n", k=KT)[:, k, cols], start=(k == 0), stop=False)
                done(nc.tensor.matmul(ps[:, 3 + half, :], ones[0:1, :], bsyn[0:1, cols], start=False, stop=True), "z_mm")

        def tile(n, it, par, no_next, no_load):
            if not no_next:
                front(n + 1, 1 - par, False)
            if not no_load:
                attend(n + 2, it + 1, par)
            wait(pe, "hid_done", n, 1)
            for j in two:
                wait(pe, "ht_ev", n - 1, j + 1)
                if j == 0 and not no_next:
                    wait(pe, "xt_ev", n + 1, 1)
                elif j == 0:
                    wait(pe, "xt_ev", n, 1)
                for i in range(4):
                    k = 4 * j + i
                    mm = nc.tensor.transpose(ps[:, 5 + j, i * P:(i + 1) * P], hid[:, k * P:(k + 1) * P], ident[:, :])
                done(mm, "ht_mm")
            wait(pe, "r2_done", n, 0)
            if isinstance(n, int) and n == 0:
                pe.wait_ge(ternary, 2)
            for k in range(FT):
                if k % 4 == 0:
                    wait(pe, "ht_ev", n, k // 4 + 1)
                nc.tensor.matmul(ps[:, 7, 0:HID], ht[:, k, :], wt[1][:, :].rearrange("p (k n) -> p k n", k=FT)[:, k, :],
                                 start=(k == 0), stop=False)
            done(nc.tensor.matmul(ps[:, 7, 0:HID], ones[0:1, :], bout[0:1, :], start=False, stop=True), "out_mm")

        def prologue():
            attend(0, 0, 0)
            front(0, 0, True)
            attend(1, 0, 1)

        tiles(pe, prologue, tile)

    def scalar(act):
        start(act)
        act.wait_ge(wl, NW)
        for i in two:
            nc.scalar.activation(tmp[i][:, :], wt[i][:, :], ACT.Abs, accum_out=asum[:, i:i + 1]).then_inc(absd, 1)

        def root(n, k, var, name, nk):
            wait(act, var, n, nk)
            done(nc.scalar.activation(sd[:, k, :], sd[:, k, :], ACT.Sqrt), name)

        def attend(n):
            for j in range(4):
                wait(act, "g_mm", n, j + 1)
                wait(act, "og_done", n, 0)
                done(nc.scalar.activation(gt[:, 4 * j:4 * j + 4, :], ps[:, j % 2, :].rearrange("p (h n) -> p h n", h=4),
                                          ACT.Sigmoid), "g_ev")

        def front(n, par):
            root(n, 0, "var", "root", 1)
            wait(act, "xt_mm", n, 1)
            done(nc.scalar.activation(x1t[:, :, :], ps[:, 5, 0:HID].rearrange("p (k n) -> p k n", k=KT), ACT.Copy), "xt_ev")
            for half in two:
                cols = slice(512 * half, 512 * half + 512)
                wait(act, "z_mm", n, half + 1)
                wait(act, "hid_done", n - 1, 0)
                done(nc.scalar.activation(z[par][:, cols], ps[:, 3 + half, :], ACT.Copy), "z_ev")
                done(nc.scalar.activation(zr[par][:, cols], ps[:, 3 + half, :], ACT.Relu), "zr_ev")

        def tile(n, it, par, no_next, no_load):
            if not no_next:
                front(n + 1, 1 - par)
            if not no_load:
                attend(n + 2)
            for j in two:
                wait(act, "ht_mm", n, j + 1)
                wait(act, "out_mm", n, 0)
                done(nc.scalar.activation(ht[:, 4 * j:4 * j + 4, :], ps[:, 5 + j, :].rearrange("p (k n) -> p k n", k=4),
                                          ACT.Copy), "ht_ev")
            for k in (1, 2):
                root(n, k, "bvar", "broot", k)

        def prologue():
            attend(0)
            front(0, 0)
            attend(1)

        tiles(act, prologue, tile)

    def vector(dve):
        start(dve)
        nc.vector.memset(ones[:, :], 1.0).then_inc(ready, 1)
        dve.wait_ge(wl, NW)
        dve.wait_ge(tot, 1)
        q = 0

        def qlink(ins):
            nonlocal q
            ins.then_inc(qstep, 1)
            q += 1
            dve.wait_ge(qstep, q)

        qlink(nc.vector.tensor_scalar(thr[:, 0, :], ps[:, 7, 0:2], 1.0 / (FF * HID), None, ALU.mult))
        qlink(nc.vector.tensor_scalar(thr[:, 1, :], thr[:, 0, :], 1e-8, 0.5, ALU.add, ALU.mult))
        qlink(nc.vector.tensor_scalar(thr[:, 2, :], thr[:, 1, :], -1.0, None, ALU.mult))
        for i in two:
            qlink(nc.vector.tensor_scalar(tmp[0][:, :], wt[i][:, :], thr[:, 1, i:i + 1], thr[:, 0, i:i + 1], ALU.is_gt, ALU.mult))
            qlink(nc.vector.tensor_scalar(tmp[1][:, :], wt[i][:, :], thr[:, 2, i:i + 1], thr[:, 0, i:i + 1], ALU.is_lt, ALU.mult))
            qlink(nc.vector.tensor_tensor(tmp[0][:, :], tmp[0][:, :], tmp[1][:, :], ALU.subtract))
            qlink(nc.vector.tensor_tensor(tmp[0][:, :], tmp[0][:, :], wt[i][:, :], ALU.subtract))
            nc.vector.tensor_tensor(wt[i][:, :], wt[i][:, :], tmp[0][:, :], ALU.add).then_inc(ternary, 1)
            dve.wait_ge(ternary, i + 1)

        def settled():
            nc.vector.memset(scrap[:, :], 0.0)

        def norm(link, src, k, n, dst, var, root, nk):
            link(nc.vector.bn_stats(stats[:, k, :], src))
            settled()
            link(nc.vector.bn_aggr(mv[:, k, :], stats[:, k, :]))
            done(nc.vector.tensor_scalar(sd[:, k, :], mv[:, k, 1:2], LN_EPS, None, ALU.add), var)
            wait(dve, root, n, nk)
            link(nc.vector.reciprocal(rs[:, k, :], sd[:, k, :]))
            return nc.vector.tensor_scalar(dst, src, mv[:, k, 0:1], rs[:, k, :], ALU.subtract, ALU.mult)

        def linker(name, n):
            s, per = n_[name]
            k = 0

            def link(ins):
                nonlocal k
                ins.then_inc(s, 1)
                k += 1
                ge(dve, s, per * n + k)

            def check():
                assert k == per, (name, k, per)
            return link, check

        def front(n, it, par):
            link, check = linker("fstep", n)
            ge(dve, ld[par], NLD * it + NLD)
            wait(dve, "attn", n, 1)
            done(nc.vector.tensor_tensor(r1[:, :], ps[:, 2, 0:HID], xr[par][:, :], ALU.add), "r1_done")
            wait(dve, "r1_done", n, 1)
            done(norm(link, r1[:, :], 0, n, x1[par][:, :], "var", "root", 1), "x1_done")
            check()

        def topk(n, par, link):
            wait(dve, "z_ev", n, 2)
            src = z[par]
            settled()
            for r in range(ROUNDS_MAX):
                link(nc.vector.max(top[:, r, :], src[:, :]))
                settled()
                if r < ROUNDS_MAX - 1:
                    link(nc.vector.match_replace(out=zw[:, :], in_to_replace=top[:, r, :], in_values=src[:, :],
                                                 imm_value=-3.0e38))
                    settled()
                    src = zw
            k = (TOPK - 1) % 8
            wait(dve, "zr_ev", n, 2)
            wait(dve, "ht_mm", n, 0)
            done(nc.vector.scalar_tensor_tensor(out=hid[:, :], in0=z[par][:, :], scalar=top[:, ROUNDS_MAX - 1, k:k + 1],
                                                in1=zr[par][:, :], op0=ALU.is_ge, op1=ALU.mult), "hid_done")

        def tile(n, it, par, no_next, no_load):
            if not no_next:
                front(n + 1, it + par, 1 - par)
            link, check = linker("bstep", n)
            topk(n, par, link)
            wait(dve, "x1_done", n, 1)
            wait(dve, "out_mm", n, 1)
            done(nc.vector.tensor_tensor(r2[:, :], ps[:, 7, 0:HID], x1[par][:, :], ALU.add), "r2_done")
            wait(dve, "r2_done", n, 1)
            link(norm(link, r2[:, :], 1, n, y2[:, :], "bvar", "broot", 1))
            link(nc.vector.tensor_tensor(y2[:, :], y2[:, :], gam[:, :], ALU.mult))
            link(nc.vector.tensor_tensor(y2[:, :], y2[:, :], bet[:, :], ALU.add))
            link(nc.vector.tensor_tensor(y2[:, :], y2[:, :], x1[par][:, :], ALU.add))
            ge(dve, st[par], 64 * it)
            done(norm(link, y2[:, :], 2, n, res[par][:, :], "bvar", "broot", 2), "res_done")
            check()

        tiles(dve, lambda: front(0, 0, 0), tile)

    def gpsimd(pool):
        start(pool)

        def gate(n, it, par):
            ge(pool, ld[par], NLD * it + NLD)
            wait(pool, "g_ev", n, 4)
            wait(pool, "attn", n, 0)
            for c in two:
                cols = slice(64 * c, 64 * c + 64)
                done(nc.gpsimd.tensor_tensor(og[:, :, cols], ot[par][:, c], gt[:, :, cols], ALU.mult), "og_done")

        def tile(n, it, par, no_next, no_load):
            if not no_load:
                gate(n + 2, it + 1, par)

        def prologue():
            gate(0, 0, 0)
            gate(1, 0, 1)

        tiles(pool, prologue, tile)

    for name, f in (("sync", sync), ("tensor", tensor), ("scalar", scalar), ("vector", vector), ("gpsimd", gpsimd)):
        block_parts[name].append(f)


def layout(**a):
    a = {n.removeprefix("L0_"): np.asarray(v) for n, v in a.items()}
    x = a["attn_x"]

    def heads(m):
        return m.T.reshape(KT, P, GROUPS, 2, P).transpose(2, 1, 0, 3, 4)

    def channels(m):
        return m.reshape(GROUPS, 2, P, -1).transpose(0, 2, 1, 3)

    wpack = np.concatenate([heads(a[f"attn_W{n}"]) for n in "avkq"], axis=3)
    cpack = np.concatenate(
        [np.concatenate([channels(a[f"attn_{n}c_w"]), channels(a[f"attn_{n}c_b"])], axis=3).reshape(GROUPS, P, 10) for n in "vkq"]
        + [channels(a["attn_ba"]).reshape(GROUPS, P, 2)], axis=2)
    out = {
        "xT": x.transpose(2, 0, 1).reshape(KT, P, B, S).transpose(1, 0, 2, 3),
        "wb": a["attn_Wb"].T.reshape(KT, P, H).transpose(1, 0, 2),
        "bb": a["attn_bb"].reshape(H, 1),
        "wpack": wpack,
        "cpack": cpack,
        "lngb": np.stack([a["attn_ln_g"], a["attn_ln_b"]], axis=1),
        "x": x,
        "wgT": a["attn_Wg"].T.reshape(KT, P, H, P).transpose(1, 0, 2, 3),
        "woT": a["attn_Wo"].T.reshape(H, P, HID).transpose(1, 0, 2),
        "wsynT": a["ffn_W_syn"].T.reshape(KT, P, FF).transpose(1, 0, 2).reshape(P, -1),
        "woutT": a["ffn_W_out"].T.reshape(FT, P, HID).transpose(1, 0, 2).reshape(P, -1),
        "bsyn": a["ffn_b_syn"].reshape(1, FF),
        "bout": a["ffn_b_out"].reshape(1, HID),
        "gam": a["ffn_gamma"].reshape(1, HID),
        "bet": a["ffn_beta"].reshape(1, HID),
    }
    return {n: np.ascontiguousarray(v) for n, v in out.items()}


def build(nc, din, out):
    group_tile = (CHUNKS, P, GROUPS, GP * CHUNK)
    scratch = {n: nc.dram_tensor("scratch_" + n, group_tile, F32, kind="Internal").ap() for n in ("nr", "ia", "ca", "k", "q")}
    scratch["nb"] = nc.dram_tensor("scratch_nb", (CHUNKS, H, B * LEAF * LEAVES), F32, kind="Internal").ap()
    scratch["g"] = nc.dram_tensor("scratch_g", (PAIRS // 4, P, 2 * CHUNK), F32, kind="Internal").ap()
    scratch["o"] = nc.dram_tensor("scratch_o", (CHUNKS, P, PAIRS, CHUNK), F32, kind="Internal").ap()
    parts = {n: [] for n in ("sync", "tensor", "scalar", "vector", "gpsimd")}
    with ExitStack() as ctx:
        ps = ctx.enter_context(nc.psum_tensor("ps", [P, 8, 512], F32))
        sem = lambda name: ctx.enter_context(nc.semaphore(name))
        with ExitStack() as mem:
            projected = project(nc, mem, sem, parts, ps, din, scratch)
        with ExitStack() as mem:
            recurred = recur(nc, mem, sem, parts, ps, din, scratch, projected)
        with ExitStack() as mem:
            finish(nc, mem, sem, parts, ps, din, scratch, out, recurred)
        block = ctx.enter_context(nc.Block())

        @block.sync
        def _(sp):
            for part in parts["sync"]:
                part(sp)

        @block.tensor
        def _(pe):
            for part in parts["tensor"]:
                part(pe)

        @block.scalar
        def _(act):
            for part in parts["scalar"]:
                part(act)

        @block.vector
        def _(dve):
            for part in parts["vector"]:
                part(dve)

        @block.gpsimd
        def _(pool):
            for part in parts["gpsimd"]:
                part(pool)


def constants():
    row = np.arange(P)
    pair, step = row // LEAF, row % LEAF
    same = pair[:, None] == pair[None, :]
    earlier = same & (step[:, None] < step[None, :])
    until = same & (step[:, None] <= step[None, :])
    return {"ident": np.eye(P, dtype=np.float32),
            "mask": np.stack([same, earlier, until], axis=1).astype(np.float32),
            "pm": (row[:, None] // CHUNK == np.arange(4)[None, :]).astype(np.float32),
            "em": (step[:, None] == np.arange(LEAF - 1)[None, :]).astype(np.float32)}


def kernel(**inputs):
    import concourse.bacc as bacc
    from concourse.bass_utils import run_bass_kernel_spmd

    nc = bacc.Bacc("TRN2", target_bir_lowering=False, num_devices=1)
    arrays = {**layout(**inputs), **constants()}
    din = {n: nc.dram_tensor(n, a.shape, F32, kind="ExternalInput").ap() for n, a in arrays.items()}
    out = nc.dram_tensor("out", (B, S, HID), F32, kind="ExternalOutput").ap()
    build(nc, din, out)
    r = run_bass_kernel_spmd(nc, [arrays], core_ids=[0])
    return r.results[0]["out"]
```

```python
from contextlib import ExitStack

import numpy as np

import concourse.bass as bass
from concourse import mybir

F32 = mybir.dt.float32
ALU = mybir.AluOpType
ACT = mybir.ActivationFunctionType
AX_X = mybir.AxisListType.X

P = 128
B, S, HID = 2, 512, 256
H = 16
PAIRS = H * B
LEAF = 4
CHUNK = 32
LEAVES = CHUNK // LEAF
CHUNKS = S // CHUNK
KT = HID // P
TAPS = 4
SCALE = float(P) ** -0.5
A_FLOOR = 1e-8
LN_EPS = 1e-5
ITEMS = LEAVES * (LEAVES + 1) // 2

GROUPS = H // 2
UNITS = ["a0", "a1", "v0", "v1", "k0", "k1", "q0", "q1"]
CONVS = UNITS[2:]
GP = 4
GCOLS = GP * S


def ge(eng, sem, value):
    if isinstance(value, int) and value <= 0:
        return
    eng.wait_ge(sem, value)


class Chain:

    def __init__(self, eng, sem, per, settle=lambda: None):
        self.eng, self.sem, self.per, self.settle = eng, sem, per, settle

    def begin(self, round_):
        self.base, self.n = round_ * self.per, 0

    def __call__(self, ins):
        ins.then_inc(self.sem, 1)
        self.n += 1
        self.eng.wait_ge(self.sem, self.base + self.n)
        self.settle()

    def end(self):
        assert self.n == self.per, (self.n, self.per)


def rounds(eng, count, body):
    body(0, True, False)
    with eng.Fori(1, count - 1) as it:
        body(it, False, False)
    body(count - 1, False, True)


def project(nc, ctx, sem, block_parts, ps, din, scratch):

    def sb(name, shape):
        return ctx.enter_context(nc.sbuf_tensor(name, shape, F32))

    xT = sb("p1_xT", [P, KT, B, S])
    w = [sb(f"p1_w{i}", [P, KT, 8, P]) for i in range(2)]
    cw = [sb(f"p1_cw{i}", [P, 32]) for i in range(2)]
    wb = sb("p1_wb", [P, KT, H])
    bb = sb("p1_bb", [H, 1])
    y = [sb(f"p1_y{i}", [P, B, S]) for i in range(3)]
    k_t = [sb(f"p1_k{i}", [P, GCOLS]) for i in range(2)]
    q_t = [sb(f"p1_q{i}", [P, GCOLS]) for i in range(2)]
    vr_t = [sb(f"p1_vr{i}", [P, GCOLS]) for i in range(2)]
    ia_t = [sb(f"p1_ia{i}", [P, GCOLS]) for i in range(2)]
    ca_t = [sb(f"p1_ca{i}", [P, GCOLS]) for i in range(2)]
    ay = sb("p1_ay", [P, GCOLS])
    j2 = sb("p1_j2", [P, GCOLS // LEAF])
    j3 = sb("p1_j3", [P, GCOLS // LEAF])
    beta = sb("p1_beta", [H, B, S])
    beta_lm = sb("p1_beta_lm", [H, CHUNKS, B, LEAF, LEAVES])

    x_loaded = sem("p1_x_loaded")
    w_loaded = [sem(f"p1_w_loaded{i}") for i in range(2)]
    taps_loaded = [sem(f"p1_taps_loaded{i}") for i in range(2)]
    projected = sem("p1_projected")
    beta_projected = sem("p1_beta_projected")
    beta_done = sem("p1_beta_done")
    beta_lm_done = sem("p1_beta_lm_done")
    sig_done = sem("p1_sig_done")
    y_done = sem("p1_y_done")
    conv_done = sem("p1_conv_done")
    silu_done = sem("p1_silu_done")
    k_scaled = sem("p1_k_scaled")
    clamped = sem("p1_clamped")
    ln_done = sem("p1_ln_done")
    guess_done = sem("p1_guess_done")
    recip_done = sem("p1_recip_done")
    dve_step = sem("p1_dve_step")
    pool_step = sem("p1_pool_step")
    pool_done = sem("p1_pool_done")
    stored = [sem(f"p1_stored{i}") for i in range(2)]
    beta_lm_stored = sem("p1_beta_lm_stored")
    NCONV = len(CONVS)

    def tt(tile, k):
        return tile[:, :].rearrange("p (n t) -> p n t", t=LEAF)[:, :, k]

    def sync(sp):
        sp.dma_start(xT[:, :, :, :], din["xT"]).then_inc(x_loaded, 16)
        sp.dma_start(wb[:, :, :], din["wb"]).then_inc(x_loaded, 16)
        sp.dma_start(bb[:, :], din["bb"]).then_inc(x_loaded, 16)

        def load_weights(g, par):
            src = din["wpack"][bass.ds(g, 1)].rearrange("g p k u c -> (g p) k u c")
            sp.dma_start(w[par][:, :, :, :], src).then_inc(w_loaded[par], 16)

        def load_taps(g, par):
            sp.dma_start(cw[par][:, :], din["cpack"][bass.ds(g, 1)].rearrange("g p n -> (g p) n")).then_inc(taps_loaded[par], 16)

        for g in range(2):
            load_weights(g, g)
            load_taps(g, g)

        def body(it, first, last):
            for par in range(2):
                g = 2 * it + par
                if not last:
                    sp.wait_ge(projected, 8 * g + 8)
                    load_weights(g + 2, par)
                for tile, name in ((k_t, "k"), (vr_t, "vr"), (ia_t, "ia"), (ca_t, "ca"), (q_t, "q")):
                    if name == "vr":
                        sp.wait_ge(pool_done, g + 1)
                    elif name == "k":
                        sp.wait_ge(k_scaled, g + 1)
                    elif name == "q":
                        sp.wait_ge(silu_done, NCONV * g + NCONV)
                    dst = scratch[name][:, :, bass.ds(g, 1), :].rearrange("c p g n -> p c (g n)")
                    sp.dma_start(dst, tile[par][:, :].rearrange("p (c n) -> p c n", c=CHUNKS)).then_inc(stored[par], 16)
                if not last:
                    load_taps(g + 2, par)
            if first:
                sp.wait_ge(beta_lm_done, B)
                sp.dma_start(scratch["beta"].rearrange("c h n -> h c n"),
                             beta_lm[:, :, :, :, :].rearrange("h c b t l -> h c (b t l)")).then_inc(beta_lm_stored, 16)

        rounds(sp, GROUPS // 2, body)

    def tensor(pe):
        pe.wait_ge(x_loaded, 48)
        for b in range(B):
            for k in range(KT):
                mm = nc.tensor.matmul(ps[0:H, 6 + b, :], wb[:, k, :], xT[:, k, b, :], start=(k == 0), stop=(k == KT - 1))
        mm.then_inc(beta_projected, 1)

        def body(it, first, last):
            for par in range(2):
                g = 2 * it + par
                pe.wait_ge(w_loaded[par], 16 * it + 16)
                for u in range(8):
                    if u in (4, 5):
                        pe.wait_ge(sig_done, 2 * g + u - 3)
                    elif u in (6, 7):
                        pe.wait_ge(conv_done, NCONV * g + u - 5)
                    elif not (first and par == 0):
                        pe.wait_ge(conv_done, NCONV * (g - 1) + u + 3)
                    elif u >= 3:
                        pe.wait_ge(beta_done, 1)
                    for b in range(B):
                        for k in range(KT):
                            mm = nc.tensor.matmul(ps[:, 2 * (u % 4) + b, :], w[par][:, k, u, :], xT[:, k, b, :],
                                                  start=(k == 0), stop=(k == KT - 1))
                    mm.then_inc(projected, 1)

        rounds(pe, GROUPS // 2, body)

    def scalar(act):
        act.wait_ge(beta_projected, 1)
        nc.scalar.activation(beta[:, :, :], ps[0:H, 6:8, :], ACT.Sigmoid, bias=bb[:, 0:1]).then_inc(beta_done, 1)

        def sigmoids(it, par):
            g = 2 * it + par
            ge(act, stored[par], 80 * it)
            act.wait_ge(taps_loaded[par], 16 * it + 16)
            for u in range(2):
                act.wait_ge(projected, 8 * g + u + 1)
                out = ca_t[par][:, :].rearrange("p (c n t) -> p n c t", c=CHUNKS, t=CHUNK)[:, B * u:B * u + B]
                nc.scalar.activation(out, ps[:, 2 * u:2 * u + 2, :].rearrange("p b (c t) -> p b c t", t=CHUNK),
                                     ACT.Sigmoid, bias=cw[par][:, 30 + u:31 + u]).then_inc(sig_done, 1)

        def tap3(it, par, n, started=True):
            g, u = 2 * it + par, n + 2
            act.wait_ge(projected, 8 * g + u + 1)
            if started:
                act.wait_ge(silu_done, NCONV * g + n - 2)
            nc.scalar.activation(y[n % 3][:, :, :], ps[:, 2 * (u % 4):2 * (u % 4) + 2, :], ACT.Identity,
                                 bias=cw[par][:, 5 * n + 4:5 * n + 5],
                                 scale=cw[par][:, 5 * n + 3:5 * n + 4]).then_inc(y_done, 1)

        def silu(it, par, n):
            act.wait_ge(conv_done, NCONV * (2 * it + par) + n + 1)
            tile = {"v": vr_t, "k": k_t, "q": q_t}[CONVS[n][0]][par]
            h = n % 2
            out = tile[:, :].rearrange("p (c n t) -> p n c t", c=CHUNKS, t=CHUNK)[:, B * h:B * h + B]
            nc.scalar.activation(out, y[n % 3][:, :, :].rearrange("p b (c t) -> p b c t", t=CHUNK),
                                 ACT.Silu).then_inc(silu_done, 1)

        def body(it, first, last):
            if first:
                sigmoids(0, 0)
                tap3(0, 0, 0, started=False)
            for par in range(2):
                g = 2 * it + par
                start = first and par == 0
                for n in range(NCONV):
                    if n + 1 < NCONV:
                        tap3(it, par, n + 1, started=not (start and n < 2))
                    elif par == 0:
                        sigmoids(it, 1)
                        tap3(it, 1, 0)
                    elif not last:
                        sigmoids(it + 1, 0)
                        tap3(it + 1, 0, 0)
                    if n == 0:
                        act.wait_ge(clamped, g + 1)
                        nc.scalar.activation(ia_t[par][:, :], ca_t[par][:, :], ACT.Ln).then_inc(ln_done, 1)
                        act.wait_ge(ln_done, g + 1)
                        nc.scalar.activation(ia_t[par][:, :], ia_t[par][:, :], ACT.Exp, scale=-1.0).then_inc(guess_done, 1)
                    if n == 4:
                        act.wait_ge(silu_done, NCONV * g + 4)
                        nc.scalar.activation(k_t[par][:, :], k_t[par][:, :], ACT.Copy, scale=-SCALE).then_inc(k_scaled, 1)
                    silu(it, par, n)

        rounds(act, GROUPS // 2, body)

    def vector(dve):
        link = Chain(dve, dve_step, 2 * (1 + 2 * NCONV))

        def reciprocal(g, par):
            dve.wait_ge(guess_done, g + 1)
            link(nc.vector.scalar_tensor_tensor(out=ay[:, :], in0=ca_t[par][:, :], scalar=-1.0, in1=ia_t[par][:, :],
                                                op0=ALU.mult, op1=ALU.mult))
            nc.vector.scalar_tensor_tensor(out=ia_t[par][:, :], in0=ay[:, :], scalar=2.0, in1=ia_t[par][:, :],
                                           op0=ALU.add, op1=ALU.mult).then_inc(recip_done, 1)

        def body(it, first, last):
            link.begin(it)
            for par in range(2):
                g = 2 * it + par
                ge(dve, stored[par], 80 * it)
                dve.wait_ge(sig_done, 2 * g + 2)
                nc.vector.tensor_scalar(ca_t[par][:, :], ca_t[par][:, :], A_FLOOR, None, ALU.max).then_inc(clamped, 1)
                for n in range(NCONV):
                    if n == 2:
                        reciprocal(g, par)
                    slot = 2 * ((n + 2) % 4)
                    dve.wait_ge(y_done, NCONV * g + n + 1)
                    for k in range(TAPS - 2, -1, -1):
                        s = TAPS - 1 - k
                        ins = nc.vector.scalar_tensor_tensor(
                            out=y[n % 3][:, :, s:S], in0=ps[:, slot:slot + 2, 0:S - s],
                            scalar=cw[par][:, 5 * n + k:5 * n + k + 1], in1=y[n % 3][:, :, s:S],
                            op0=ALU.mult, op1=ALU.add)
                        if k:
                            link(ins)
                        else:
                            ins.then_inc(conv_done, 1)
            link.end()

        rounds(dve, GROUPS // 2, body)

    def gpsimd(pool):
        pool.wait_ge(beta_done, 1)
        for b in range(B):
            nc.gpsimd.tensor_scalar(beta_lm[:, :, b, :, :], beta[:, b, :].rearrange("h (c l t) -> h c t l", l=LEAVES, t=LEAF),
                                    1.0, None, ALU.mult).then_inc(beta_lm_done, 1)
        link = Chain(pool, pool_step, 2 * 5)

        def body(it, first, last):
            link.begin(it)
            for par in range(2):
                g = 2 * it + par
                ia, ca, vr = ia_t[par], ca_t[par], vr_t[par]
                mul = lambda o, a, b: nc.gpsimd.tensor_tensor(o, a, b, ALU.mult)
                ge(pool, pool_done, g)
                pool.wait_ge(recip_done, g + 1)
                link(mul(j2[:, :], tt(ia, 0), tt(ia, 1)))
                link(mul(j3[:, :], j2[:, :], tt(ia, 2)))
                for k in range(1, LEAF):
                    link(mul(tt(ca, k), tt(ca, k - 1), tt(ca, k)))
                pool.wait_ge(silu_done, NCONV * g + 2)
                mul(tt(vr, 1), tt(vr, 1), tt(ia, 0))
                mul(tt(vr, 2), tt(vr, 2), j2[:, :])
                mul(tt(vr, 3), tt(vr, 3), j3[:, :]).then_inc(pool_done, 1)
            link.end()

        rounds(pool, GROUPS // 2, body)

    def finished(eng):
        for par in range(2):
            eng.wait_ge(stored[par], 80 * (GROUPS // 2))
        eng.wait_ge(beta_lm_stored, 16)

    for name, f in (("sync", sync), ("tensor", tensor), ("scalar", scalar), ("vector", vector), ("gpsimd", gpsimd)):
        block_parts[name].append(f)
    return finished


POOL_SHARE = 9


def item(src, leaf):
    return src * LEAVES - src * (src - 1) // 2 + leaf - src


def recur(nc, ctx, sem, block_parts, ps, din, scratch, start, early):

    def sb(name, shape):
        return ctx.enter_context(nc.sbuf_tensor("p2_" + name, shape, F32))

    two = range(2)
    ia_st, ca_st, vr_st = (sb(n, [P, PAIRS, CHUNK]) for n in ("ia", "ca", "vr"))
    gc = sb("gc", [P, PAIRS // 4, 2, CHUNK])
    gx = sb("gx", [P, LEAVES, 2, CHUNK])
    lm = sb("lm", [P, LEAVES, P])
    g = [sb(f"g{i}", [P, ITEMS, 2 * P]) for i in two]
    kq_st = [sb("kq0", [P, 2, PAIRS, CHUNK])]
    kt, vr_lm, nd = ([sb(f"{n}0", [P, LEAVES, P])] for n in ("kt", "vr_lm", "nd"))
    kq_st.append(sb("kq1", [P, 2, PAIRS, CHUNK]))
    for tiles_, n in ((kt, "kt"), (vr_lm, "vr_lm"), (nd, "nd")):
        tiles_.append(sb(n + "1", [P, LEAVES, P]))
    beta_st = [sb(f"beta{i}", [P, LEAVES]) for i in two]
    u = [sb(f"u{i}", [P, LEAVES, P]) for i in two]
    state = sb("state", [P, PAIRS, P])
    xs = sb("xs", [P, 2, LEAVES, P])
    us = [xs[:, 0], xs[:, 1]]
    ut = sb("ut", [P, PAIRS, CHUNK])
    at, al = ([sb(f"{n}{i}", [P, LEAVES, P]) for i in two] for n in ("at", "al"))
    o = [sb(f"o{i}", [P, LEAVES, P]) for i in two]
    oc = sb("oc", [P, PAIRS, CHUNK])
    wm = sb("wm", [P, P])
    w = [sb(f"w{i}", [P, P]) for i in two]
    ab = [sb(f"ab{i}", [P, LEAVES, PAIRS]) for i in two]
    e = [sb(f"e{i}", [P, LEAVES, PAIRS]) for i in two]
    stats = sb("stats", [P, LEAVES, 6])
    mv = sb("mv", [P, LEAVES, 2])
    std, rstd, nmr = (sb(n, [P, LEAVES]) for n in ("std", "rstd", "nmr"))
    ident = sb("ident", [P, P])
    mask = sb("mask", [P, 3, P])
    em = sb("em", [P, LEAF - 1])
    scrap = sb("scrap", [1, 1])
    lngb = sb("lngb", [P, 2])
    pm = sb("pm", [P, 4])

    PK = [ps[:, 0, 0:P], ps[:, 1, 0:P]]
    PQ = [ps[:, 2, 0:P], ps[:, 3, 0:P]]
    GB = 4
    AUX = [6, 7]
    UPB = [0, 1, 4, 5]
    SPREADS = [(s, a, min(a + 4, LEAVES), q) for s in range(LEAVES) for a in range(s + 1, LEAVES, 4) for q in two]
    SPREADS, POOL_SPREADS = SPREADS[:-POOL_SHARE], SPREADS[-POOL_SHARE:]
    NG = len(SPREADS)
    G_FROM = [NG * max(0, l - 2) // (LEAVES - 2) for l in range(LEAVES + 1)]
    PREP = [("nd", 0), ("nd", 1), ("kt", 0), ("at", 0), ("at", 1), ("kt", 1), ("al", 0), ("al", 1)]

    n_ = {}
    for name, per in dict(x_mm=4, xs_ready=8, xv_ready=LEAVES - 1, pk=4 * LEAVES, wm_ready=3 * LEAVES, w_ready=LEAVES, u_ready=LEAVES - 1,
                          ud=LEAVES - 2, pq=LEAVES, o_done=LEAVES, bn_done=LEAVES, ag_done=LEAVES, wt_mm=LEAVES,
                          wt_ev=LEAVES, ab_mm=LEAVES, ab_ev=LEAVES, prep_mm=8, prep_ev=8, gc_mm=1, gc_ev=1, g_stored=16, g_loaded=16 * LEAF, g_ev=NG, gd_ev=LEAVES + POOL_SHARE, t2_mm=2,
                          us_ev=8, up_mm=8, up_ev=8, ot_mm=4, ot_ev=4, norm=LEAVES, var_ready=1, sq_ready=1,
                          rs_ready=1, nm_ready=1, ring_ready=3, vrlm_ready=1, pool_prep=1,
                          oc_stored=16, pool_step=2 * LEAVES - 2).items():
        n_[name] = (sem("p2_" + name), per)
    ldk = [sem(f"p2_ldk{i}") for i in two]
    ldg = sem("p2_ldg")
    consts = sem("p2_consts")
    zeroed = sem("p2_zeroed")
    NCONST = 5 * 16

    def wait(eng, name, c, k):
        s, per = n_[name]
        ge(eng, s, per * c + k)

    def done(ins, name):
        ins.then_inc(n_[name][0], 1)

    def rounds2(eng, prologue, chunk, epilogue):
        prologue()

        def body(it, first, last):
            for par in two:
                chunk(2 * it + par, it, par, first and par == 0, last and par == 1, last)

        rounds(eng, CHUNKS // 2, body)
        epilogue()

    def spreading(par, s, a, b, q):
        dst = g[par][:, item(s, a):item(s, a) + b - a, q * P:(q + 1) * P].rearrange("p l (n t) -> p l n t", t=LEAF)
        src = gx[:, s, q, LEAF * a:LEAF * b].rearrange("p (l t) -> p l t", t=LEAF).unsqueeze(2)
        own = mask[:, 0:1, :].rearrange("p o (n t) -> p o n t", t=LEAF)
        return dst, src.broadcast_to([P, b - a, PAIRS, LEAF]), own.broadcast_to([P, b - a, PAIRS, LEAF])

    def sync(sp):
        start(sp)
        for dst, src in ((ident[:, :], din["ident"]), (mask[:, :, :], din["mask"]), (em[:, :], din["em"]), (pm[:, :], din["pm"]),
                         (lngb[:, :], din["lngb"])):
            sp.dma_start(dst, src).then_inc(consts, 16)

        def at_chunk(name, c):
            return scratch[name][bass.ds(c, 1)]

        def load_kq(c, par):
            for j, name in enumerate(("k", "q")):
                sp.dma_start(kq_st[par][:, j, :, :], at_chunk(name, c).rearrange("c p g (n t) -> (c p) (g n) t", t=CHUNK)
                             ).then_inc(ldk[par], 16)
            sp.dma_start(beta_st[par][:, :], at_chunk("beta", c).rearrange("c h (m l) -> (c h m) l", l=LEAVES)
                         ).then_inc(ldk[par], 16)

        def regroup(n):
            wait(sp, "gc_ev", n, 1)
            sp.dma_start(scratch["g"].rearrange("g r n -> r g n"), gc[:, :, :, :].rearrange("p g q t -> p g (q t)")
                         ).then_inc(n_["g_stored"][0], 16)
            wait(sp, "g_stored", n, 16)
            for t in range(LEAF):
                src = scratch["g"].rearrange("g (f l t) n -> t (g f) l n", f=4, t=LEAF)[t]
                sp.dma_start(gx[t::LEAF, :, :, :].rearrange("p l q t -> p l (q t)"), src).then_inc(n_["g_loaded"][0], 16)

        def load_gates(c):
            for tile, name in ((ia_st, "ia"), (ca_st, "ca"), (vr_st, "vr")):
                sp.dma_start(tile[:, :, :], at_chunk(name, c).rearrange("c p g (n t) -> (c p) (g n) t", t=CHUNK)
                             ).then_inc(ldg, 16)

        def store(m):
            wait(sp, "ot_ev", m, 4)
            sp.dma_start(scratch["o"][bass.ds(m, 1)].rearrange("c p n t -> (c p) n t"), oc[:, :, :]
                         ).then_inc(n_["oc_stored"][0], 16)

        def prologue():
            load_kq(0, 0)
            load_gates(0)
            load_kq(1, 1)
            regroup(0)
            wait(sp, "pool_prep", 0, 1)
            wait(sp, "ring_ready", 0, 3)
            wait(sp, "vrlm_ready", 0, 1)
            load_gates(1)

        def chunk(c, it, par, first, no_next, no_load):
            if not no_load:
                wait(sp, "x_mm", c, 4)
                load_kq(c + 2, par)
            if not no_next:
                regroup(c + 1)
            else:
                wait(sp, "ring_ready", c, 3)
                wait(sp, "vrlm_ready", c, 1)
                wait(sp, "pool_prep", c, 1)
                wait(sp, "prep_mm", c, 8)
                wait(sp, "g_ev", c, NG)
                wait(sp, "gd_ev", c, LEAVES + POOL_SHARE)
                wait(sp, "pq", c - 1, LEAVES)
                wait(sp, "up_mm", c - 1, 8)
                wait(sp, "w_ready", c - 1, LEAVES)
                early["weights"](sp)
            if not no_load:
                wait(sp, "pool_prep", c + 1, 1)
                wait(sp, "ring_ready", c + 1, 3)
                wait(sp, "vrlm_ready", c + 1, 1)
                load_gates(c + 2)
            if not first:
                store(c - 1)

        def epilogue():
            wait(sp, "pq", CHUNKS - 1, LEAVES)
            wait(sp, "oc_stored", 3, 16)
            early["tiles"](sp)
            store(CHUNKS - 1)

        rounds2(sp, prologue, chunk, epilogue)

    def gpsimd(pool):
        start(pool)
        nc.gpsimd.memset(state[:, :, :], 0.0).then_inc(zeroed, 1)
        for i in two:
            nc.gpsimd.memset(ab[i][:, 0, :], 1.0).then_inc(zeroed, 1)
        pool.wait_ge(zeroed, 3)
        pool.wait_ge(consts, NCONST)

        def prep(n, par):
            mul = lambda o_, a, b: nc.gpsimd.tensor_tensor(o_, a, b, ALU.mult)
            ge(pool, ldg, 48 * n + 48)
            wait(pool, "wt_ev", n - 2, LEAVES)
            wait(pool, "xs_ready", n - 2, 8)
            wait(pool, "ab_mm", n - 2, LEAVES)
            a_of = lambda l: ca_st[:, :, :].rearrange("p n (l t) -> p l n t", t=LEAF)[:, l, :, LEAF - 1]
            s, per = n_["pool_step"]
            k = 0

            def link(ins):
                nonlocal k
                ins.then_inc(s, 1)
                k += 1
                pool.wait_ge(s, per * n + k)

            link(mul(e[par][:, LEAVES - 1, :], a_of(LEAVES - 1), ab[par][:, 0, :]))
            for l in range(1, LEAVES):
                link(mul(ab[par][:, l, :], ab[par][:, l - 1, :], a_of(l - 1)))
                ins = mul(e[par][:, LEAVES - 1 - l, :], e[par][:, LEAVES - l, :], a_of(LEAVES - 1 - l))
                if l < LEAVES - 1:
                    link(ins)
                else:
                    done(ins, "pool_prep")
            assert k == per, (k, per)
            wait(pool, "g_loaded", n, 16 * LEAF)
            wait(pool, "pq", n - 2, LEAVES)
            for l in range(LEAVES):
                src = gx[:, l, :, LEAF * l:LEAF * l + LEAF].unsqueeze(2).broadcast_to([P, 2, PAIRS, LEAF])
                dst = g[par][:, item(l, l), :].rearrange("p (q n t) -> p q n t", q=2, t=LEAF)
                done(mul(dst, src, mask[:, 1:3, :].rearrange("p q (n t) -> p q n t", t=LEAF)), "gd_ev")
            for one in POOL_SPREADS:
                dst, src, own = spreading(par, *one)
                done(mul(dst, src, own), "gd_ev")

        def chunk(c, it, par, first, no_next, no_load):
            wait(pool, "xs_ready", c, 8)
            wait(pool, "vrlm_ready", c, 1)
            for l in range(1, LEAVES):
                done(nc.gpsimd.tensor_tensor(xs[:, 0, l, :], xs[:, 0, l, :], vr_lm[par][:, l, :], ALU.add), "xv_ready")
            if not no_next:
                prep(c + 1, 1 - par)

        rounds2(pool, lambda: prep(0, 0), chunk, lambda: None)

    def tensor(pe):
        start(pe)
        pe.wait_ge(consts, NCONST)
        hist = []

        def aux(name, c, k):
            if len(hist) >= 2:
                wait(pe, *hist[-2])
            bank = AUX[aux.n % 2]
            aux.n += 1
            hist.append((name, c, k))
            return bank

        aux.n = 0

        def G(par, s, l, q):
            return g[par][:, item(s, l), q * P:(q + 1) * P]

        def products(n, it2, par):
            ge(pe, ldk[par], 48 * it2 + 48)
            wait(pe, "gc_ev", n, 0)
            for p in range(PAIRS):
                mm = nc.tensor.matmul(ps[32 * (p % 4):32 * (p % 4) + 32, GB, 64 * (p // 4):64 * (p // 4) + 64],
                                      kq_st[par][:, 0, p, :], kq_st[par][:, :, p, :], start=True, stop=True)
            done(mm, "gc_mm")

        def prep_job(n, par, j):
            b = aux("prep_ev", n, j + 1)
            kind, half = PREP[j]
            if kind != "kt":
                wait(pe, "ring_ready", n, ("nd", "at", "al").index(kind) + 1)
                tiles = [lm[:, 4 * half + i, :] for i in range(4)]
            else:
                ks = kq_st[par][:, 0].rearrange("p n t -> p (n t)")
                tiles = [ks[:, P * i:P * i + P] for i in range(4 * half, 4 * half + 4)]
            for i, t in enumerate(tiles):
                mm = nc.tensor.transpose(ps[:, b, i * P:(i + 1) * P], t, ident[:, :])
            done(mm, "prep_mm")

        def acc(bank, lhsT, rhs):
            return nc.tensor.matmul(bank, lhsT, rhs, start=False, stop=True, skip_group_check=True)

        def out_job(m, k):
            b = aux("ot_ev", m, k + 1)
            wait(pe, "norm", m, 2 * k + 2)
            for i in two:
                mm = nc.tensor.transpose(ps[:, b, i * P:(i + 1) * P], o_of(m)[:, 2 * k + i, :], ident[:, :])
            done(mm, "ot_mm")

        parity = {}

        def o_of(m):
            return parity["prev_o"]

        def prologue():
            pe.wait_ge(ldk[0], 48)
            products(0, 0, 0)
            for j in range(8):
                prep_job(0, 0, j)
            pe.wait_ge(zeroed, 3)

        def chunk(c, it, par, first, no_next, no_load):
            n = c + 1
            if not first:
                hist[:] = [("us_ev", c - 1, 8), ("us_ev", c - 1, 8)]
            aux.n = 0
            parity["prev_o"] = o[1 - par]
            for j in range(4):
                b = aux("xs_ready", c, 2 * j + 2)
                wait(pe, "up_ev", c - 1, 8)
                bank = ps[:, b, :].rearrange("p (n q t) -> p q n t", n=8, q=2)
                for p in range(8):
                    n2 = min(p + 2, 8)
                    mm = nc.tensor.matmul(bank[:, :, p:n2, :], state[:, 8 * j + p, :],
                                          kq_st[par][:, :, 8 * j + p:8 * j + n2, :], start=True, stop=True)
                done(mm, "x_mm")

            def base_k(l):
                wait(pe, "w_ready", c, l - 1)
                if l:
                    wait(pe, "xv_ready", c, l)
                    return nc.tensor.transpose(PK[l % 2], xs[:, 0, l, :], ident[:, :])
                nc.tensor.transpose(PK[l % 2], vr_lm[par][:, l, :], ident[:, :])
                return acc(PK[l % 2], xs[:, 0, l, :], ident[:, :])

            def base_q(l):
                wait(pe, "o_done", c, l - 1)
                nc.tensor.transpose(PQ[l % 2], xs[:, 1, l, :], ident[:, :])

            if not no_next:
                prep_job(n, 1 - par, 0)
            wait(pe, "xs_ready", c, 8)
            wait(pe, "vrlm_ready", c, 1)
            done(base_k(0), "pk")
            base_q(0)
            wait(pe, "g_ev", c, NG)
            wait(pe, "gd_ev", c, LEAVES + POOL_SHARE)
            for l in range(LEAVES):
                more = l + 1 < LEAVES
                uv = u[(l + 1) % 2]
                if more:
                    base_k(l + 1)
                if l >= 1 and not no_next:
                    b = aux("wt_ev", c, l)
                    nc.tensor.transpose(ps[:, b, 0:P], w[(l - 1) % 2][:, :], ident[:, :]).then_inc(n_["wt_mm"][0], 1)
                wait(pe, "wm_ready", c, 3 * l + 1)
                done(acc(PK[l % 2], G(par, l, l, 0), wm[:, :]), "pk")
                if not no_next:
                    if l >= 1:
                        prep_job(n, 1 - par, l)
                    b = aux("ab_ev", c, l + 1)
                    for i in range(4):
                        mm = nc.tensor.transpose(ps[:, b, i * P:(i + 1) * P],
                                                 e[par][:, 0, 4 * l + i:4 * l + i + 1].broadcast_to([P, P]), ident[:, :])
                    done(mm, "ab_mm")
                wait(pe, "wm_ready", c, 3 * l + 2)
                done(acc(PK[l % 2], G(par, l, l, 0), wm[:, :]), "pk")
                if more and l >= 1:
                    wait(pe, "ud", c, l)
                    for s in range(l):
                        acc(PK[(l + 1) % 2], G(par, s, l + 1, 0), uv[:, s, :])
                if not no_next and l == 0:
                    products(n, it + par, 1 - par)
                wait(pe, "wm_ready", c, 3 * l + 3)
                done(acc(PK[l % 2], G(par, l, l, 0), wm[:, :]), "pk")
                if more:
                    base_q(l + 1)
                    for s in range(l):
                        acc(PQ[(l + 1) % 2], G(par, s, l + 1, 1), uv[:, s, :])
                if l >= 4 and not first:
                    out_job(c - 1, l - 4)
                if no_next and l == 5:
                    early["total"](pe)
                if more:
                    wait(pe, "u_ready", c, l + 1)
                    done(acc(PK[(l + 1) % 2], G(par, l, l + 1, 0), uv[:, l, :]), "pk")
                elif not no_next:
                    b = aux("wt_ev", c, LEAVES)
                    wait(pe, "w_ready", c, LEAVES)
                    nc.tensor.transpose(ps[:, b, 0:P], w[l % 2][:, :], ident[:, :]).then_inc(n_["wt_mm"][0], 1)
                wait(pe, "w_ready", c, l + 1)
                done(acc(PQ[l % 2], G(par, l, l, 1), w[l % 2][:, :]), "pq")
                if more:
                    acc(PQ[(l + 1) % 2], G(par, l, l + 1, 1), uv[:, l, :])
            if no_next:
                return
            uf = ut[:, :, :].rearrange("p n t -> p (n t)")
            for j in two:
                b = aux("us_ev", c, 7 + j)
                wait(pe, "wt_ev", c, LEAVES)
                for i in range(4):
                    mm = nc.tensor.transpose(ps[:, b, i * P:(i + 1) * P], uf[:, (4 * j + i) * P:(4 * j + i + 1) * P],
                                             ident[:, :])
                done(mm, "t2_mm")
            wait(pe, "gc_ev", n, 1)
            for r in range(8):
                p4, half = r // 2, r % 2
                wait(pe, "us_ev", c, r + 1)
                if r >= 4:
                    wait(pe, "up_ev", c, r - 3)
                for i in range(4):
                    mm = nc.tensor.matmul(ps[:, UPB[r % 4], i * P:(i + 1) * P], kt[par][:, 4 * half + i, :],
                                          us[p4 % 2][:, 4 * half + i, :], start=True, stop=True)
                done(mm, "up_mm")

        def epilogue():
            wait(pe, "o_done", CHUNKS - 1, LEAVES)
            early["gates"](pe)
            parity["prev_o"] = o[(CHUNKS - 1) % 2]
            aux.n = 0
            for k in range(4):
                out_job(CHUNKS - 1, k)

        rounds2(pe, prologue, chunk, epilogue)

    def vector(dve):
        start(dve)
        dve.wait_ge(consts, NCONST)
        dve.wait_ge(zeroed, 3)
        mul = lambda o_, a, b: nc.vector.tensor_tensor(o_, a, b, ALU.mult)

        def spread(n, par, lo, hi):
            for s, a, b, q in SPREADS[lo:hi]:
                if lo == 0:
                    wait(dve, "g_loaded", n, 16 * LEAF)
                dst, src, own = spreading(par, s, a, b, q)
                done(mul(dst, src, own), "g_ev")

        def outputs(c, par, l, first):
            wait(dve, "pq", c, l + 1)
            if l == 0:
                wait(dve, "ot_mm", c - 2, 4)
            done(mul(o[par][:, l, :], PQ[l % 2], at[par][:, l, :]), "o_done")
            wait(dve, "o_done", c, l + 1)
            done(nc.vector.bn_stats(stats[:, l, :], o[par][:, l, :]), "bn_done")

        def turned(c, par, l):
            wait(dve, "wt_mm", c, l + 1)
            wt = ps[:, aux_of[("wt", l)], 0:P].rearrange("p (n t) -> p n t", t=LEAF)
            done(mul(ut[:, :, LEAF * l:LEAF * l + LEAF], wt,
                     e[par][:, l, :].unsqueeze(2).broadcast_to([P, PAIRS, LEAF])), "wt_ev")

        def norm_scalars(m):
            wait(dve, "sq_ready", m, 1)
            wait(dve, "norm", m, 0)
            done(nc.vector.reciprocal(rstd[:, :], std[:, :]), "rs_ready")
            wait(dve, "rs_ready", m, 1)
            done(nc.vector.scalar_tensor_tensor(out=nmr[:, :], in0=mv[:, :, 0], scalar=-1.0, in1=rstd[:, :],
                                                op0=ALU.mult, op1=ALU.mult), "nm_ready")

        def variance(c):
            wait(dve, "bn_done", c, LEAVES)
            nc.vector.memset(scrap[:, :], 0.0)
            for l in range(LEAVES):
                done(nc.vector.bn_aggr(mv[:, l, :], stats[:, l, :]), "ag_done")
            wait(dve, "ag_done", c, LEAVES)
            done(nc.vector.tensor_scalar(std[:, :], mv[:, :, 1], LN_EPS, None, ALU.add), "var_ready")

        aux_of = {}

        def prologue():
            spread(0, 0, 0, NG)

        def chunk(c, it, par, first, no_next, no_load):
            n = c + 1
            aux_of.clear()
            aux_of.update(aux_banks(first, no_next))
            if no_next:
                early["ones"](dve)
            for j in range(4):
                wait(dve, "x_mm", c, j + 1)
                if j == 0:
                    wait(dve, "pool_prep", c, 1)
                bank = ps[:, aux_of[("x", j)], :].rearrange("p (n q l t) -> p q l n t", n=8, q=2, t=LEAF)
                for q in two:
                    done(mul(xs[:, q, :, 32 * j:32 * j + 32].rearrange("p l (n t) -> p l n t", t=LEAF), bank[:, q],
                             ab[par][:, :, 8 * j:8 * j + 8].unsqueeze(3).broadcast_to([P, LEAVES, 8, LEAF])), "xs_ready")
            if first:
                wait(dve, "prep_ev", 0, 8)
            else:
                wait(dve, "prep_ev", c, 8)
            for l in range(LEAVES):
                more = l + 1 < LEAVES
                for m in range(LEAF - 1):
                    wait(dve, "pk", c, 4 * l + m + 1)
                    done(nc.vector.scalar_tensor_tensor(out=wm[:, :], in0=PK[l % 2], scalar=em[:, m:m + 1],
                                                        in1=nd[par][:, l, :], op0=ALU.mult, op1=ALU.mult), "wm_ready")
                    if m == 0 and more and l >= 1:
                        wait(dve, "u_ready", c, l)
                        wait(dve, "ud", c, l - 1)
                        wait(dve, "pq", c, l)
                        done(mul(u[(l + 1) % 2][:, 0:l, :], u[l % 2][:, 0:l, :],
                                 al[par][:, l:l + 1, :].broadcast_to([P, l, P])), "ud")
                    if m == 0 and l >= 1 and not no_next:
                        turned(c, par, l - 1)
                    if m == 1 and l >= 1:
                        outputs(c, par, l - 1, first)
                    if m == 1 and l == 1 and not first:
                        norm_scalars(c - 1)
                    if m == 2 and not no_next:
                        wait(dve, "ab_mm", c, l + 1)
                        done(mul(state[:, 4 * l:4 * l + 4, :], state[:, 4 * l:4 * l + 4, :],
                                 ps[:, aux_of[("ab", l)], :].rearrange("p (n i) -> p n i", n=4)), "ab_ev")
                wait(dve, "pk", c, 4 * l + 4)
                done(mul(w[l % 2][:, :], PK[l % 2], nd[par][:, l, :]), "w_ready")
                if more:
                    wait(dve, "w_ready", c, l + 1)
                    done(mul(u[(l + 1) % 2][:, l, :], w[l % 2][:, :], al[par][:, l, :]), "u_ready")
                if not no_next:
                    spread(n, 1 - par, G_FROM[l], G_FROM[l + 1])
            if not no_next:
                turned(c, par, LEAVES - 1)
            outputs(c, par, LEAVES - 1, first)
            variance(c)
            if no_next:
                return
            wait(dve, "ab_ev", c, LEAVES)
            by4 = state[:, :, :].rearrange("p (n f) i -> p n f i", f=4)
            for r in range(8):
                wait(dve, "up_mm", c, r + 1)
                st = by4[:, 4 * (r % 2):4 * (r % 2) + 4, r // 2, :]
                done(nc.vector.tensor_tensor(st, st, ps[:, UPB[r % 4], :].rearrange("p (n i) -> p n i", n=4),
                                             ALU.add), "up_ev")

        def epilogue():
            early["ternary"](dve, 0)
            norm_scalars(CHUNKS - 1)
            early["ternary"](dve, 1)

        rounds2(dve, prologue, chunk, epilogue)

    def scalar(act):
        start(act)
        act.wait_ge(consts, NCONST)
        aux_of = {}

        def prep_read(n, it2, par, j, bank):
            wait(act, "prep_mm", n, j + 1)
            if j == 0:
                wait(act, "o_done", n - 2, LEAVES)
                wait(act, "up_mm", n - 2, 8)
            src = ps[:, bank, :].rearrange("p (n i) -> p n i", n=4)
            kind, half = PREP[j]
            part = slice(4 * half, 4 * half + 4)
            if kind == "nd":
                for i in range(4):
                    l = 4 * half + i
                    ins = nc.scalar.activation(nd[par][:, l, :], src[:, i, :], ACT.Copy, scale=beta_st[par][:, l:l + 1])
            else:
                tile = dict(at=at, al=al, kt=kt)[kind]
                ins = nc.scalar.activation(tile[par][:, part, :], src, ACT.Copy, scale=-1.0 if kind == "kt" else 1.0)
            done(ins, "prep_ev")

        def by_leaf(tile):
            return tile.rearrange("p n (l t) -> p l n t", t=LEAF)

        def to_leaves(dst, src, name):
            done(nc.scalar.activation(dst[:, :, :].rearrange("p l (n t) -> p l n t", t=LEAF), src, ACT.Copy), name)

        def prep_step(n, it2, par, j, bank):
            if j == 0:
                ge(act, ldk[par], 48 * it2 + 48)
                ge(act, ldg, 48 * n + 48)
                wait(act, "prep_mm", n - 1, 8)
                to_leaves(lm, by_leaf(ia_st[:, :, :]), "ring_ready")
            prep_read(n, it2, par, j, bank)
            if j == 0:
                wait(act, "gc_mm", n, 1)
                wait(act, "g_stored", n, 0)
                done(nc.scalar.activation(gc[:, :, :, :].rearrange("p g q t -> p (g q t)"), ps[:, GB, :], ACT.Copy), "gc_ev")
            if j == 1:
                wait(act, "prep_mm", n, 2)
                to_leaves(lm, by_leaf(ca_st[:, :, :]), "ring_ready")
            if j == 2:
                wait(act, "pk", n - 2, 4 * LEAVES)
                to_leaves(vr_lm[par], by_leaf(vr_st[:, :, :]), "vrlm_ready")
            if j == 4:
                wait(act, "prep_mm", n, 5)
                last = by_leaf(ca_st[:, :, :])[:, :, :, LEAF - 1:LEAF]
                to_leaves(lm, last.broadcast_to([P, LEAVES, PAIRS, LEAF]), "ring_ready")

        def root(m):
            wait(act, "var_ready", m, 1)
            done(nc.scalar.activation(std[:, :], std[:, :], ACT.Sqrt), "sq_ready")

        def normalise(m, tile, lo, hi):
            wait(act, "nm_ready", m, 1)
            for l in range(lo, hi):
                done(nc.scalar.activation(tile[:, l, :], tile[:, l, :], ACT.Identity, scale=rstd[:, l:l + 1],
                                          bias=nmr[:, l:l + 1]), "norm")

        def out_read(m, k, bank):
            wait(act, "ot_mm", m, k + 1)
            if k == 0:
                wait(act, "oc_stored", m, 0)
            dst = oc[:, :, :].rearrange("p n (l t) -> p l n t", t=LEAF)[:, 2 * k:2 * k + 2]
            done(nc.scalar.activation(dst, ps[:, bank, 0:2 * P].rearrange("p (l n t) -> p l n t", l=2, t=LEAF),
                                      ACT.Identity, scale=lngb[:, 0:1], bias=lngb[:, 1:2]), "ot_ev")

        def prologue():
            for j in range(8):
                prep_step(0, 0, 0, j, AUX[j % 2])

        def chunk(c, it, par, first, no_next, no_load):
            aux_of.clear()
            aux_of.update(aux_banks(first, no_next))
            for l in range(LEAVES):
                if not no_next:
                    prep_step(c + 1, it + par, 1 - par, l, aux_of[("prep", l)])
                if not first:
                    if l == 0:
                        root(c - 1)
                    if 1 <= l < 4:
                        normalise(c - 1, o[1 - par], (0, 3, 6)[l - 1], (3, 6, 8)[l - 1])
                    if l >= 4:
                        out_read(c - 1, l - 4, aux_of[("ot", l - 4)])
                if no_next and l == 3:
                    wait(act, "up_mm", c - 1, 8)
                    wait(act, "w_ready", c - 1, LEAVES)
                    early["magnitudes"](act)
            for r in range(0 if no_next else 8):
                p4, half = r // 2, r % 2
                if r < 2:
                    wait(act, "t2_mm", c, r + 1)
                if r >= 4:
                    wait(act, "up_mm", c, r - 3)
                done(nc.scalar.activation(us[p4 % 2][:, 4 * half:4 * half + 4, :],
                                          ps[:, aux_of[("t2", half)], :].rearrange("p (n i) -> p n i", n=4),
                                          ACT.Copy, scale=pm[:, p4:p4 + 1]), "us_ev")

        def epilogue():
            early["sigmoids"](act)
            root(CHUNKS - 1)
            normalise(CHUNKS - 1, o[(CHUNKS - 1) % 2], 0, LEAVES)
            for k in range(4):
                out_read(CHUNKS - 1, k, AUX[k % 2])

        rounds2(act, prologue, chunk, epilogue)

    def aux_jobs(first, no_next):
        jobs = [("x", j) for j in range(4)]
        for l in range(LEAVES):
            if not no_next:
                if l >= 1:
                    jobs.append(("wt", l - 1))
                jobs += [("prep", l), ("ab", l)]
            if l >= 4 and not first:
                jobs.append(("ot", l - 4))
        if not no_next:
            jobs += [("wt", LEAVES - 1), ("t2", 0), ("t2", 1)]
        return jobs

    assert all(len(aux_jobs(*kind)) % 2 == 0 for kind in ((True, False), (False, False), (False, True)))

    def aux_banks(first, no_next):
        return {job: AUX[i % 2] for i, job in enumerate(aux_jobs(first, no_next))}

    for name, f in (("sync", sync), ("tensor", tensor), ("scalar", scalar), ("vector", vector), ("gpsimd", gpsimd)):
        block_parts[name].append(f)

    def finished(eng):
        eng.wait_ge(n_["oc_stored"][0], 16 * CHUNKS)
    return finished


TILES = B * S // P
FF = 1024
TOPK = max(1, int(FF * (1.0 - 0.9)))
FT = FF // P
HALF = TOPK // 2
ROUNDS_HI, ROUNDS_LO = (TOPK + 7) // 8, (HALF + 7) // 8
ROUNDS_ALL = ROUNDS_HI + ROUNDS_LO
VAR_AT, NORM_AT, RESULT_AT = 4, 7, 9


def finish(nc, ctx, sem, block_parts, ps, din, scratch, out, start, early):

    def sb(name, shape):
        return ctx.enter_context(nc.sbuf_tensor("p3_" + name, shape, F32))

    two = range(2)
    wo = sb("wo", [P, H, HID])
    bsyn = sb("bsyn", [1, FF])
    wg = sb("wg", [P, KT, H, P])
    wt = [sb("wsyn", [P, 2048]), sb("wout", [P, 2048])]
    bout = sb("bout", [1, HID])
    gam, bet = sb("gam", [P, HID]), sb("bet", [P, HID])
    ident = sb("ident", [P, P])
    xr = [sb(f"xr{i}", [P, HID]) for i in two]
    ot = [sb(f"ot{i}", [P, 2, H, B * CHUNK]) for i in two]
    gt = sb("gt", [P, H, P])
    og = sb("og", [P, H, P])
    r1 = sb("r1", [P, HID])
    x1t = sb("x1t", [P, KT, P])
    top = sb("top", [P, 8 * ROUNDS_ALL])
    stats, mv, sd, rs = (sb(n, [P, 3, k]) for n, k in (("stats", 6), ("mv", 2), ("sd", 1), ("rs", 1)))
    tmp = [sb(f"tmp{i}", [P, 2048]) for i in two]
    ones = sb("ones", [P, P])
    xt = [sb(f"xt{i}", [P, KT, P]) for i in two]
    asum = sb("asum", [P, 2])
    thr = sb("thr", [P, 3, 2])
    x1 = [sb(f"x1{i}", [P, HID]) for i in two]
    z = [sb(f"z{i}", [P, FF]) for i in two]
    zr = [sb(f"zr{i}", [P, FF]) for i in two]
    zp = sb("zp", [P, 2, FF // 2])
    zw = [sb(f"zw{i}", [P, FF // 2]) for i in two]
    both = sb("both", [P, HALF])
    last = sb("last", [P, 8])
    least = sb("least", [P, 1])
    scrap = sb("scrap", [1, 2])
    hid = sb("hid", [P, FF])
    ht = sb("ht", [P, FT, P])
    r2, y2 = sb("r2", [P, HID]), sb("y2", [P, HID])
    res = [sb(f"res{i}", [P, HID]) for i in two]

    n_ = {}
    for name, per in dict(g_mm=4, g_ev=4, og_done=2, attn=1, r1_done=1, x1_done=1, xt_mm=1, xt_ev=1, z_mm=2, z_ev=2,
                          zr_ev=2, hid_done=1, ht_mm=2, ht_ev=2, out_mm=1, r2_done=1, var=1, root=1, bvar=2, broot=2,
                          res_done=1, fstep=3, tstep=2 + 2 * ROUNDS_ALL - 2 + 3, bstep=10).items():
        n_[name] = (sem("p3_" + name), per)
    wl = sem("p3_weights")
    ffl = sem("p3_ff_weights")
    ldx = [sem(f"p3_ldx{i}") for i in two]
    ld = [sem(f"p3_ld{i}") for i in two]
    st = sem("p3_st")
    absd, tot, ready, qstep, ternary = (sem("p3_" + n) for n in ("absd", "tot", "ready", "qstep", "ternary"))
    loads = [(wg[:, :, :, :], "wgT"), (wo[:, :, :], "woT"),
             (bsyn[:, :], "bsyn"), (bout[:, :], "bout"), (gam[:, :], "gam"), (bet[:, :], "bet"), (ident[:, :], "ident")]
    NW = 16 * len(loads)

    def wait(eng, name, n, k):
        s, per = n_[name]
        ge(eng, s, per * n + k)

    def done(ins, name):
        ins.then_inc(n_[name][0], 1)

    def tiles(eng, prologue, tile, epilogue=lambda: None):
        prologue()

        def body(it, first, last):
            for par in two:
                tile(2 * it + par, it, par, last and par == 1, last)

        rounds(eng, TILES // 2, body)
        epilogue()

    def before(n):
        return None if isinstance(n, int) and n == 0 else n - 1

    def load_weights(sp):
        for i, name in enumerate(("wsynT", "woutT")):
            sp.dma_start(wt[i][:, :], din[name]).then_inc(ffl, 16)
        for dst, name in loads:
            src = din[name]
            if name in ("gam", "bet"):
                src = src.broadcast_to([P, HID])
            sp.dma_start(dst, src).then_inc(wl, 16)
            if name == "wgT":
                for n in two:
                    load_turned(sp, n, n)

    early["weights"] = load_weights

    def load_turned(sp, n, par):
        xsrc = din["xT"].rearrange("p k b (n c t) -> n p k c b t", c=2, t=CHUNK)
        for c in two:
            for k in range(KT):
                sp.dma_start(xt[par][:, k, c * 64:c * 64 + 64].rearrange("p (b t) -> p b t", b=B),
                             xsrc[bass.ds(n, 1), :, k, c].rearrange("n p b t -> (n p) b t")).then_inc(ldx[par], 16)

    def load(sp, n, par):
        for c in two:
            sp.dma_start(ot[par][:, c, :, :], scratch["o"].rearrange("(n c) p (h b) t -> n c p h (b t)", c=2, b=B)
                         [bass.ds(n, 1), c].rearrange("n p h t -> (n p) h t")).then_inc(ld[par], 16)
            for b in range(B):
                sp.dma_start(xr[par][c * 64 + b * 32:c * 64 + b * 32 + 32, :],
                             din["x"].rearrange("b (n c t) d -> b c n t d", c=2, t=CHUNK)[b, c, bass.ds(n, 1)]
                             .rearrange("n t d -> (n t) d")).then_inc(ld[par], 16)

    def first_tiles(sp):
        load(sp, 0, 0)
        load(sp, 1, 1)

    early["tiles"] = first_tiles

    def sync(sp):
        start(sp)

        def free(n):
            wait(sp, "r1_done", n, 1)
            wait(sp, "og_done", n, 2)
            wait(sp, "g_mm", n, 4)

        def store(n, par):
            wait(sp, "res_done", n, 1)
            for c in two:
                for b in range(B):
                    sp.dma_start(out.rearrange("b (n c t) d -> b c n t d", c=2, t=CHUNK)[b, c, bass.ds(n, 1)]
                                 .rearrange("n t d -> (n t) d"),
                                 res[par][c * 64 + b * 32:c * 64 + b * 32 + 32, :]).then_inc(st, 16)

        def tile(n, it, par, no_next, no_load):
            if par == 0 and not no_load:
                free(n)
                load_turned(sp, n + 2, 0)
                load(sp, n + 2, 0)
                free(n + 1)
                load_turned(sp, n + 3, 1)
                load(sp, n + 3, 1)
            if before(n) is not None:
                store(n - 1, 1 - par)

        tiles(sp, lambda: None, tile, lambda: store(TILES - 1, 1))
        sp.wait_ge(st, 64 * TILES)

    NLDX, NLD = 16 * 4, 16 * 6

    def total(pe):
        pe.wait_ge(ready, 1)
        pe.wait_ge(absd, 2)
        nc.tensor.matmul(ps[:, 4, 0:2], ones[:, :], asum[:, :], start=True, stop=True).then_inc(tot, 1)

    def gates(pe, n, it, par):
        ge(pe, ldx[par], NLDX * it + NLDX)
        for j in range(4):
            wait(pe, "g_ev", n, j - 1)
            for i in range(4):
                for k in range(KT):
                    mm = nc.tensor.matmul(ps[:, j % 2, i * P:(i + 1) * P], wg[:, k, 4 * j + i, :], xt[par][:, k, :],
                                          start=(k == 0), stop=(k == KT - 1))
            done(mm, "g_mm")

    def attention_out(pe, n):
        wait(pe, "og_done", n, 2)
        wait(pe, "r1_done", n, 0)
        for h in range(H):
            mm = nc.tensor.matmul(ps[:, 2, 0:HID], og[:, h, :], wo[:, h, :], start=(h == 0), stop=(h == H - 1))
        done(mm, "attn")

    def first_gates(pe):
        pe.wait_ge(wl, NW)
        gates(pe, 0, 0, 0)
        attention_out(pe, 0)

    early["total"] = total
    early["gates"] = first_gates

    def tensor(pe):
        def front(n, par, first):
            wait(pe, "x1_done", n, 1)
            if not (isinstance(n, int) and n < 2):
                wait(pe, "ht_ev", n - 2, 1)
            for k in range(KT):
                mm = nc.tensor.transpose(ps[:, 5, k * P:(k + 1) * P], x1[par][:, k * P:(k + 1) * P], ident[:, :])
            done(mm, "xt_mm")
            wait(pe, "xt_ev", n, 1)
            if first:
                pe.wait_ge(ternary, 1)
            for half in two:
                wait(pe, "zr_ev", n - 1, half + 1)
                cols = slice(512 * half, 512 * half + 512)
                for k in range(KT):
                    nc.tensor.matmul(ps[:, 3 + half, :], x1t[:, k, :],
                                     wt[0][:, :].rearrange("p (k n) -> p k n", k=KT)[:, k, cols], start=(k == 0), stop=False)
                done(nc.tensor.matmul(ps[:, 3 + half, :], ones[0:1, :], bsyn[0:1, cols], start=False, stop=True), "z_mm")

        def back(n, last):
            wait(pe, "hid_done", n, 1)
            for j in two:
                wait(pe, "ht_ev", n - 1, j + 1)
                if j == 0:
                    wait(pe, "xt_ev", n if last else n + 1, 1)
                for i in range(4):
                    k = 4 * j + i
                    mm = nc.tensor.transpose(ps[:, 5 + j, i * P:(i + 1) * P], hid[:, k * P:(k + 1) * P], ident[:, :])
                done(mm, "ht_mm")
            wait(pe, "r2_done", n, 0)
            if isinstance(n, int) and n == 0:
                pe.wait_ge(ternary, 2)
            for k in range(FT):
                if k % 4 == 0:
                    wait(pe, "ht_ev", n, k // 4 + 1)
                nc.tensor.matmul(ps[:, 7, 0:HID], ht[:, k, :], wt[1][:, :].rearrange("p (k n) -> p k n", k=FT)[:, k, :],
                                 start=(k == 0), stop=False)
            done(nc.tensor.matmul(ps[:, 7, 0:HID], ones[0:1, :], bout[0:1, :], start=False, stop=True), "out_mm")

        def tile(n, it, par, no_next, no_load):
            if before(n) is not None:
                back(n - 1, False)
            if not no_load:
                gates(pe, n + 2, it + 1, par)
            if not no_next:
                front(n + 1, 1 - par, False)
            if not no_load:
                attention_out(pe, n + 2)

        def prologue():
            gates(pe, 1, 0, 1)
            start(pe)
            front(0, 0, True)
            attention_out(pe, 1)

        tiles(pe, prologue, tile, lambda: back(TILES - 1, True))

    def magnitudes(act):
        act.wait_ge(ffl, 32)
        for i in two:
            nc.scalar.activation(tmp[i][:, :], wt[i][:, :], ACT.Abs, accum_out=asum[:, i:i + 1]).then_inc(absd, 1)

    def attend(act, n):
        for j in range(4):
            wait(act, "g_mm", n, j + 1)
            wait(act, "og_done", n, 0)
            done(nc.scalar.activation(gt[:, 4 * j:4 * j + 4, :], ps[:, j % 2, :].rearrange("p (h n) -> p h n", h=4),
                                      ACT.Sigmoid), "g_ev")

    early["magnitudes"] = magnitudes
    early["sigmoids"] = lambda act: attend(act, 0)

    def scalar(act):
        attend(act, 1)
        start(act)

        def root(n, k, var, name, nk):
            wait(act, var, n, nk)
            done(nc.scalar.activation(sd[:, k, :], sd[:, k, :], ACT.Sqrt), name)

        def scores(n, par):
            wait(act, "xt_mm", n, 1)
            done(nc.scalar.activation(x1t[:, :, :], ps[:, 5, 0:HID].rearrange("p (k n) -> p k n", k=KT), ACT.Copy), "xt_ev")
            for half in two:
                cols = slice(512 * half, 512 * half + 512)
                wait(act, "z_mm", n, half + 1)
                wait(act, "hid_done", n - 1, 0)
                done(nc.scalar.activation(z[par][:, cols], ps[:, 3 + half, :], ACT.Copy), "z_ev")
                done(nc.scalar.activation(zr[par][:, cols], ps[:, 3 + half, :], ACT.Relu), "zr_ev")

        def hidden(n):
            for j in two:
                wait(act, "ht_mm", n, j + 1)
                wait(act, "out_mm", n, 0)
                done(nc.scalar.activation(ht[:, 4 * j:4 * j + 4, :], ps[:, 5 + j, :].rearrange("p (k n) -> p k n", k=4),
                                          ACT.Copy), "ht_ev")

        def tile(n, it, par, no_next, no_load):
            if before(n) is not None:
                hidden(n - 1)
            if not no_load:
                attend(act, n + 2)
            if before(n) is not None:
                root(n - 1, 1, "bvar", "broot", 1)
            if not no_next:
                root(n + 1, 0, "var", "root", 1)
            if before(n) is not None:
                root(n - 1, 2, "bvar", "broot", 2)
            if not no_next:
                scores(n + 1, 1 - par)

        def prologue():
            root(0, 0, "var", "root", 1)
            scores(0, 0)

        def epilogue():
            hidden(TILES - 1)
            for k in (1, 2):
                root(TILES - 1, k, "bvar", "broot", k)

        tiles(act, prologue, tile, epilogue)

    def set_ones(dve):
        nc.vector.memset(ones[:, :], 1.0).then_inc(ready, 1)

    def make_ternary(dve, i):
        q = 7 * i

        def qlink(ins):
            nonlocal q
            ins.then_inc(qstep, 1)
            q += 1
            dve.wait_ge(qstep, q)

        if i == 0:
            dve.wait_ge(ffl, 32)
            dve.wait_ge(tot, 1)
            qlink(nc.vector.tensor_scalar(thr[:, 0, :], ps[:, 4, 0:2], 1.0 / (FF * HID), None, ALU.mult))
            qlink(nc.vector.tensor_scalar(thr[:, 1, :], thr[:, 0, :], 1e-8, 0.5, ALU.add, ALU.mult))
            qlink(nc.vector.tensor_scalar(thr[:, 2, :], thr[:, 1, :], -1.0, None, ALU.mult))
        qlink(nc.vector.tensor_scalar(tmp[0][:, :], wt[i][:, :], thr[:, 1, i:i + 1], thr[:, 0, i:i + 1], ALU.is_gt, ALU.mult))
        qlink(nc.vector.tensor_scalar(tmp[1][:, :], wt[i][:, :], thr[:, 2, i:i + 1], thr[:, 0, i:i + 1], ALU.is_lt, ALU.mult))
        qlink(nc.vector.tensor_tensor(tmp[0][:, :], tmp[0][:, :], tmp[1][:, :], ALU.subtract))
        qlink(nc.vector.tensor_tensor(tmp[0][:, :], tmp[0][:, :], wt[i][:, :], ALU.subtract))
        nc.vector.tensor_tensor(wt[i][:, :], wt[i][:, :], tmp[0][:, :], ALU.add).then_inc(ternary, 1)
        dve.wait_ge(ternary, i + 1)

    early["ones"] = set_ones
    early["ternary"] = make_ternary

    def vector(dve):
        start(dve)
        dve.wait_ge(wl, NW)

        def settled(n, k=0):
            if not isinstance(n, int):
                nc.vector.memset(scrap[:, k:k + 1], 0.0)

        def variance(link, src, k, n, var):
            link(nc.vector.bn_stats(stats[:, k, :], src))
            settled(n)
            link(nc.vector.bn_aggr(mv[:, k, :], stats[:, k, :]))
            done(nc.vector.tensor_scalar(sd[:, k, :], mv[:, k, 1:2], LN_EPS, None, ALU.add), var)

        def normed(link, src, k, n, dst, root, nk):
            wait(dve, root, n, nk)
            link(nc.vector.reciprocal(rs[:, k, :], sd[:, k, :]))
            return nc.vector.tensor_scalar(dst, src, mv[:, k, 0:1], rs[:, k, :], ALU.subtract, ALU.mult)

        def linker(name, n):
            s, per = n_[name]
            k = 0

            def link(ins, lag=0):
                nonlocal k
                ins.then_inc(s, 1)
                k += 1
                ge(dve, s, per * n + k - lag)

            def check():
                assert k == per, (name, k, per)
            return link, check

        def front_variance(link, n, it, par):
            ge(dve, ld[par], NLD * it + NLD)
            wait(dve, "attn", n, 1)
            done(nc.vector.tensor_tensor(r1[:, :], ps[:, 2, 0:HID], xr[par][:, :], ALU.add), "r1_done")
            wait(dve, "r1_done", n, 1)
            variance(link, r1[:, :], 0, n, "var")

        def front_normed(link, n, par):
            done(normed(link, r1[:, :], 0, n, x1[par][:, :], "root", 1), "x1_done")

        def back_variance(link, n, par):
            wait(dve, "x1_done", n, 1)
            wait(dve, "out_mm", n, 1)
            done(nc.vector.tensor_tensor(r2[:, :], ps[:, 7, 0:HID], x1[par][:, :], ALU.add), "r2_done")
            wait(dve, "r2_done", n, 1)
            variance(link, r2[:, :], 1, n, "bvar")

        def back_normed(link, n, par):
            link(normed(link, r2[:, :], 1, n, y2[:, :], "broot", 1))
            link(nc.vector.tensor_tensor(y2[:, :], y2[:, :], gam[:, :], ALU.mult))
            link(nc.vector.tensor_tensor(y2[:, :], y2[:, :], bet[:, :], ALU.add))
            link(nc.vector.tensor_tensor(y2[:, :], y2[:, :], x1[par][:, :], ALU.add))
            variance(link, y2[:, :], 2, n, "bvar")

        def back_result(link, n, par):
            ge(dve, st, 64 * n)
            done(normed(link, y2[:, :], 2, n, res[par][:, :], "broot", 2), "res_done")

        def largest(link, n, par, lo, hi):
            if lo == 0:
                wait(dve, "z_ev", n, 2)
                for k, op in enumerate((ALU.max, ALU.min)):
                    link(nc.vector.tensor_tensor(zp[:, k, :], z[par][:, 0:FF // 2], z[par][:, FF // 2:FF], op), 1)
                settled(n, 1)
            for r in range(lo, hi):
                searches = [(0, 0)] if r >= ROUNDS_LO else [(0, 0), (1, ROUNDS_HI)]
                for k, at in searches:
                    src = zp[:, k, :] if r == 0 else zw[k][:, :]
                    link(nc.vector.max(top[:, 8 * (at + r):8 * (at + r) + 8], src), len(searches) - 1)
                    if r + 1 != ROUNDS_HI:
                        settled(n, k)
                if r + 1 == ROUNDS_LO:
                    searches.pop()
                for k, at in searches if r + 1 != ROUNDS_HI else []:
                    src = zp[:, k, :] if r == 0 else zw[k][:, :]
                    link(nc.vector.match_replace(out=zw[k][:, :], in_to_replace=top[:, 8 * (at + r):8 * (at + r) + 8],
                                                 in_values=src, imm_value=-3.0e38), len(searches) - 1)
                    settled(n, k)

        def threshold(link, n):
            greater = top[:, TOPK - 1 - HALF:TOPK - 1][:, ::-1]
            lesser = top[:, 8 * ROUNDS_HI:8 * ROUNDS_HI + HALF]
            link(nc.vector.tensor_tensor(both[:, :], greater, lesser, ALU.min))
            settled(n)
            link(nc.vector.max(last[:, :], both[:, :]))
            link(nc.vector.tensor_tensor(least[:, :], last[:, 0:1], top[:, TOPK - 1:TOPK], ALU.max))

        def tile(n, it, par, no_next, no_load):
            tlink, tcheck = linker("tstep", n)
            flink, fcheck = linker("fstep", n + 1)
            blink, bcheck = linker("bstep", n - 1)
            ends = before(n) is not None
            largest(tlink, n, par, 0, VAR_AT)
            if ends:
                back_variance(blink, n - 1, 1 - par)
            if not no_next:
                front_variance(flink, n + 1, it + par, 1 - par)
            largest(tlink, n, par, VAR_AT, NORM_AT)
            if ends:
                back_normed(blink, n - 1, 1 - par)
            if not no_next:
                front_normed(flink, n + 1, 1 - par)
                fcheck()
            largest(tlink, n, par, NORM_AT, RESULT_AT)
            if ends:
                back_result(blink, n - 1, 1 - par)
                bcheck()
            largest(tlink, n, par, RESULT_AT, ROUNDS_HI)
            threshold(tlink, n)
            tcheck()
            wait(dve, "zr_ev", n, 2)
            wait(dve, "ht_mm", n, 0)
            done(nc.vector.scalar_tensor_tensor(out=hid[:, :], in0=z[par][:, :], scalar=least[:, 0:1],
                                                in1=zr[par][:, :], op0=ALU.is_ge, op1=ALU.mult), "hid_done")

        def prologue():
            flink, fcheck = linker("fstep", 0)
            front_variance(flink, 0, 0, 0)
            front_normed(flink, 0, 0)
            fcheck()

        def epilogue():
            blink, bcheck = linker("bstep", TILES - 1)
            back_variance(blink, TILES - 1, 1)
            back_normed(blink, TILES - 1, 1)
            back_result(blink, TILES - 1, 1)
            bcheck()

        tiles(dve, prologue, tile, epilogue)

    def gpsimd(pool):
        def gate(n, it, par):
            ge(pool, ld[par], NLD * it + NLD)
            wait(pool, "g_ev", n, 4)
            wait(pool, "attn", n, 0)
            for c in two:
                cols = slice(64 * c, 64 * c + 64)
                done(nc.gpsimd.tensor_tensor(og[:, :, cols], ot[par][:, c], gt[:, :, cols], ALU.mult), "og_done")

        def tile(n, it, par, no_next, no_load):
            if not no_load:
                gate(n + 2, it + 1, par)

        def prologue():
            gate(0, 0, 0)
            start(pool)
            gate(1, 0, 1)

        tiles(pool, prologue, tile)

    for name, f in (("sync", sync), ("tensor", tensor), ("scalar", scalar), ("vector", vector), ("gpsimd", gpsimd)):
        block_parts[name].append(f)


def layout(**a):
    a = {n.removeprefix("L0_"): np.asarray(v) for n, v in a.items()}
    x = a["attn_x"]

    def heads(m):
        return m.T.reshape(KT, P, GROUPS, 2, P).transpose(2, 1, 0, 3, 4)

    def channels(m):
        return m.reshape(GROUPS, 2, P, -1).transpose(0, 2, 1, 3)

    wpack = np.concatenate([heads(a[f"attn_W{n}"]) for n in "avkq"], axis=3)
    cpack = np.concatenate(
        [np.concatenate([channels(a[f"attn_{n}c_w"]), channels(a[f"attn_{n}c_b"])], axis=3).reshape(GROUPS, P, 10) for n in "vkq"]
        + [channels(a["attn_ba"]).reshape(GROUPS, P, 2)], axis=2)
    out = {
        "xT": x.transpose(2, 0, 1).reshape(KT, P, B, S).transpose(1, 0, 2, 3),
        "wb": a["attn_Wb"].T.reshape(KT, P, H).transpose(1, 0, 2),
        "bb": a["attn_bb"].reshape(H, 1),
        "wpack": wpack,
        "cpack": cpack,
        "lngb": np.stack([a["attn_ln_g"], a["attn_ln_b"]], axis=1),
        "x": x,
        "wgT": a["attn_Wg"].T.reshape(KT, P, H, P).transpose(1, 0, 2, 3),
        "woT": a["attn_Wo"].T.reshape(H, P, HID).transpose(1, 0, 2),
        "wsynT": a["ffn_W_syn"].T.reshape(KT, P, FF).transpose(1, 0, 2).reshape(P, -1),
        "woutT": a["ffn_W_out"].T.reshape(FT, P, HID).transpose(1, 0, 2).reshape(P, -1),
        "bsyn": a["ffn_b_syn"].reshape(1, FF),
        "bout": a["ffn_b_out"].reshape(1, HID),
        "gam": a["ffn_gamma"].reshape(1, HID),
        "bet": a["ffn_beta"].reshape(1, HID),
    }
    return {n: np.ascontiguousarray(v) for n, v in out.items()}


def build(nc, din, out):
    group_tile = (CHUNKS, P, GROUPS, GP * CHUNK)
    scratch = {n: nc.dram_tensor("scratch_" + n, group_tile, F32, kind="Internal").ap() for n in ("vr", "ia", "ca", "k", "q")}
    scratch["beta"] = nc.dram_tensor("scratch_beta", (CHUNKS, H, B * LEAF * LEAVES), F32, kind="Internal").ap()
    scratch["g"] = nc.dram_tensor("scratch_g", (PAIRS // 4, P, 2 * CHUNK), F32, kind="Internal").ap()
    scratch["o"] = nc.dram_tensor("scratch_o", (CHUNKS, P, PAIRS, CHUNK), F32, kind="Internal").ap()
    parts = {n: [] for n in ("sync", "tensor", "scalar", "vector", "gpsimd")}
    with ExitStack() as ctx:
        ps = ctx.enter_context(nc.psum_tensor("ps", [P, 8, 512], F32))
        sem = lambda name: ctx.enter_context(nc.semaphore(name))
        early = {}
        with ExitStack() as mem:
            projected = project(nc, mem, sem, parts, ps, din, scratch)
        with ExitStack() as mem:
            recurred = recur(nc, mem, sem, parts, ps, din, scratch, projected, early)
        with ExitStack() as mem:
            finish(nc, mem, sem, parts, ps, din, scratch, out, recurred, early)
        block = ctx.enter_context(nc.Block())

        @block.sync
        def _(sp):
            for part in parts["sync"]:
                part(sp)

        @block.tensor
        def _(pe):
            for part in parts["tensor"]:
                part(pe)

        @block.scalar
        def _(act):
            for part in parts["scalar"]:
                part(act)

        @block.vector
        def _(dve):
            for part in parts["vector"]:
                part(dve)

        @block.gpsimd
        def _(pool):
            for part in parts["gpsimd"]:
                part(pool)


def constants():
    row = np.arange(P)
    pair, step = row // LEAF, row % LEAF
    same = pair[:, None] == pair[None, :]
    earlier = same & (step[:, None] < step[None, :])
    until = same & (step[:, None] <= step[None, :])
    return {"ident": np.eye(P, dtype=np.float32),
            "mask": -np.stack([same, earlier, until], axis=1).astype(np.float32),
            "pm": (row[:, None] // CHUNK == np.arange(4)[None, :]).astype(np.float32),
            "em": (step[:, None] == np.arange(LEAF - 1)[None, :]).astype(np.float32)}


def kernel(**inputs):
    import concourse.bacc as bacc
    from concourse.bass_utils import run_bass_kernel_spmd

    nc = bacc.Bacc("TRN2", target_bir_lowering=False, num_devices=1)
    arrays = {**layout(**inputs), **constants()}
    din = {n: nc.dram_tensor(n, a.shape, F32, kind="ExternalInput").ap() for n, a in arrays.items()}
    out = nc.dram_tensor("out", (B, S, HID), F32, kind="ExternalOutput").ap()
    build(nc, din, out)
    r = run_bass_kernel_spmd(nc, [arrays], core_ids=[0])
    return r.results[0]["out"]
```
